# Optimizing a Trainium2 kernel written in Bass

```python
import numpy as np
import jax
import jax.numpy as jnp

def _softmax(x, axis=-1):
    return jax.nn.softmax(x, axis=axis)

def _gelu(x):
    return jax.nn.gelu(x, approximate=True)

def _silu(x):
    return jax.nn.silu(x)

def _sigmoid(x):
    return jax.nn.sigmoid(x)

def _layernorm(x, axis=-1, eps=1e-05):
    m = jnp.mean(x, axis=axis, keepdims=True)
    v = jnp.var(x, axis=axis, keepdims=True)
    return (x - m) / jnp.sqrt(v + eps)

def _scatter_add(tgt, idx, src, axis=0):
    return tgt.at[idx].add(src)

def _segment_sum(src, seg, n):
    return jax.ops.segment_sum(src, seg, n)
kernel_name = 'mk_gnn_resnorm_d2_gnn_r8_998bb6'

def setup_inputs(seed: int=0):
    np.random.seed(seed)
    _w = jnp.asarray

    def _rec_inputs():
        import jax
        import jax.numpy as jnp
        _gk = jax.random.key(seed)
        x = -0.0006008 + 1.001 * jax.random.normal(jax.random.fold_in(_gk, 1), (6250, 256), jnp.float32)
        _s = jax.random.randint(jax.random.fold_in(_gk, 2), (50000,), 0, 6250, jnp.int32)
        _d = jax.random.randint(jax.random.fold_in(_gk, 3), (50000,), 0, 6250, jnp.int32)
        _loop = jnp.arange(6250, dtype=jnp.int32)
        src = jnp.concatenate([_s, _d, _loop])
        dst = jnp.concatenate([_d, _s, _loop])
        _o = jnp.argsort(dst, stable=True)
        src = src[_o]
        dst = dst[_o]
        return (x, src, dst)
    x, src, dst = _rec_inputs()

    def _L0_gnn_setup():
        import jax, jax.numpy as jnp
        import numpy as np
        EPS = 1e-05
        N_NODES = 1250
        N_EDGES = 40000
        D_IN = 256
        D_OUT = 256
        key = jax.random.key(seed)
        k_x, k_e, k_wl, k_bl, k_wr = jax.random.split(key, 5)
        x = jax.random.normal(k_x, (N_NODES, D_IN), dtype=jnp.float32)
        edge_index = jax.random.randint(k_e, (2, N_EDGES), 0, N_NODES, dtype=jnp.int64)
        gamma = jnp.ones((D_IN,), dtype=jnp.float32)
        beta = jnp.zeros((D_IN,), dtype=jnp.float32)
        s = 1.0 / np.sqrt(D_IN)
        W_l = jax.random.uniform(k_wl, (D_OUT, D_IN), dtype=jnp.float32, minval=-s, maxval=s)
        b_l = jax.random.uniform(k_bl, (D_OUT,), dtype=jnp.float32, minval=-s, maxval=s)
        W_r = jax.random.uniform(k_wr, (D_OUT, D_IN), dtype=jnp.float32, minval=-s, maxval=s)
        return {'x': x, 'edge_index': edge_index, 'gamma': gamma, 'beta': beta, 'W_l': W_l, 'b_l': b_l, 'W_r': W_r}
    _L0_gnn_all = _L0_gnn_setup()
    _L0_gnn_in = {k: v for k, v in _L0_gnn_all.items() if k in ('gamma', 'beta', 'W_l', 'b_l', 'W_r')}
    del _L0_gnn_all

    def _L1_gnn_setup():
        import jax, jax.numpy as jnp
        import numpy as np
        N_NODES = 6250
        N_EDGES = 100000
        D_IN = 256
        D_HID = 256
        D_OUT = 256

        def _sage_conv(x, src, dst, Wl, bl, Wr, num_nodes):
            msg = x[src]
            agg = jax.ops.segment_sum(msg, dst, num_segments=num_nodes)
            deg = jax.ops.segment_sum(jnp.ones((src.shape[0],), x.dtype), dst, num_segments=num_nodes)
            mean = agg / jnp.maximum(deg, 1.0)[:, None]
            return jnp.einsum('nd,od->no', mean, Wl) + bl + jnp.einsum('nd,od->no', x, Wr)
        key = jax.random.key(seed)
        ks = jax.random.split(key, 12)
        x = jax.random.normal(ks[0], (N_NODES, D_IN), dtype=jnp.float32)
        edge_index = jax.random.randint(ks[1], (2, N_EDGES), 0, N_NODES, dtype=jnp.int32)

        def lin(k, dout, din):
            return jax.random.normal(k, (dout, din), dtype=jnp.float32) * (1.0 / np.sqrt(din))
        return {'x': x, 'edge_index': edge_index, 'W1l': lin(ks[2], D_HID, D_IN), 'b1l': jnp.zeros((D_HID,), jnp.float32), 'W1r': lin(ks[3], D_HID, D_IN), 'W2l': lin(ks[4], D_HID, D_HID), 'b2l': jnp.zeros((D_HID,), jnp.float32), 'W2r': lin(ks[5], D_HID, D_HID), 'W3l': lin(ks[6], D_OUT, D_HID), 'b3l': jnp.zeros((D_OUT,), jnp.float32), 'W3r': lin(ks[7], D_OUT, D_HID)}
    _L1_gnn_all = _L1_gnn_setup()
    _L1_gnn_in = {k: v for k, v in _L1_gnn_all.items() if k in ('W1l', 'b1l', 'W1r', 'W2l', 'b2l', 'W2r', 'W3l', 'b3l', 'W3r')}
    del _L1_gnn_all
    return {'x': x, 'src': src, 'dst': dst, 'L0_gnn_gamma': _L0_gnn_in['gamma'], 'L0_gnn_beta': _L0_gnn_in['beta'], 'L0_gnn_W_l': _L0_gnn_in['W_l'], 'L0_gnn_b_l': _L0_gnn_in['b_l'], 'L0_gnn_W_r': _L0_gnn_in['W_r'], 'L1_gnn_W1l': _L1_gnn_in['W1l'], 'L1_gnn_b1l': _L1_gnn_in['b1l'], 'L1_gnn_W1r': _L1_gnn_in['W1r'], 'L1_gnn_W2l': _L1_gnn_in['W2l'], 'L1_gnn_b2l': _L1_gnn_in['b2l'], 'L1_gnn_W2r': _L1_gnn_in['W2r'], 'L1_gnn_W3l': _L1_gnn_in['W3l'], 'L1_gnn_b3l': _L1_gnn_in['b3l'], 'L1_gnn_W3r': _L1_gnn_in['W3r']}

def reference(x, src, dst, L0_gnn_gamma, L0_gnn_beta, L0_gnn_W_l, L0_gnn_b_l, L0_gnn_W_r, L1_gnn_W1l, L1_gnn_b1l, L1_gnn_W1r, L1_gnn_W2l, L1_gnn_b2l, L1_gnn_W2r, L1_gnn_W3l, L1_gnn_b3l, L1_gnn_W3r):
    import jax
    import jax.numpy as jnp

    def _L0_gnn_ref(x, edge_index, gamma, beta, W_l, b_l, W_r):
        import jax, jax.numpy as jnp
        import numpy as np
        EPS = 1e-05
        N_NODES = 1250
        N_EDGES = 40000
        D_IN = 256
        D_OUT = 256
        mu = jnp.mean(x, axis=-1, keepdims=True)
        var = jnp.mean(jnp.square(x - mu), axis=-1, keepdims=True)
        h = (x - mu) * jax.lax.rsqrt(var + EPS) * gamma + beta
        h = jax.nn.relu(h)
        src, dst = (edge_index[0], edge_index[1])
        n = h.shape[0]
        msg = h[src]
        summed = jax.ops.segment_sum(msg, dst, num_segments=n)
        deg = jax.ops.segment_sum(jnp.ones((src.shape[0],), dtype=h.dtype), dst, num_segments=n)
        agg = summed / jnp.maximum(deg, 1.0)[:, None]
        return agg @ W_l.T + b_l + h @ W_r.T

    def _L1_gnn_ref(x, edge_index, W1l, b1l, W1r, W2l, b2l, W2r, W3l, b3l, W3r):
        import jax, jax.numpy as jnp
        import numpy as np
        N_NODES = 6250
        N_EDGES = 100000
        D_IN = 256
        D_HID = 256
        D_OUT = 256

        def _sage_conv(x, src, dst, Wl, bl, Wr, num_nodes):
            msg = x[src]
            agg = jax.ops.segment_sum(msg, dst, num_segments=num_nodes)
            deg = jax.ops.segment_sum(jnp.ones((src.shape[0],), x.dtype), dst, num_segments=num_nodes)
            mean = agg / jnp.maximum(deg, 1.0)[:, None]
            return jnp.einsum('nd,od->no', mean, Wl) + bl + jnp.einsum('nd,od->no', x, Wr)
        src, dst = (edge_index[0], edge_index[1])
        n = x.shape[0]
        h = _sage_conv(x, src, dst, W1l, b1l, W1r, n)
        h = jax.nn.relu(h)
        h = _sage_conv(h, src, dst, W2l, b2l, W2r, n)
        h = jax.nn.relu(h)
        h = _sage_conv(h, src, dst, W3l, b3l, W3r, n)
        return h
    edge_index = jnp.stack([src, dst])
    x = _layernorm(x + _L0_gnn_ref(x, edge_index, L0_gnn_gamma, L0_gnn_beta, L0_gnn_W_l, L0_gnn_b_l, L0_gnn_W_r), axis=-1)
    x = _layernorm(x + _L1_gnn_ref(x, edge_index, L1_gnn_W1l, L1_gnn_b1l, L1_gnn_W1r, L1_gnn_W2l, L1_gnn_b2l, L1_gnn_W2r, L1_gnn_W3l, L1_gnn_b3l, L1_gnn_W3r), axis=-1)
    return x

_drawn_inputs = setup_inputs


def setup_inputs(seed=0):
    import zlib

    import numpy as np

    out = dict(_drawn_inputs(seed))
    spreads = {'L0_gnn_gamma': (1.0, 0.2),
     'L0_gnn_beta': (0.0, 0.1),
     'L1_gnn_b1l': (0.0, 0.1),
     'L1_gnn_b2l': (0.0, 0.1),
     'L1_gnn_b3l': (0.0, 0.1)}
    factors = {}
    for name, (base, spread) in spreads.items():
        noise = np.random.default_rng([zlib.crc32(name.encode()), seed]).standard_normal(out[name].shape)
        drawn = base * np.exp(spread * noise) if base else spread * noise
        out[name] = jnp.asarray(drawn.astype(out[name].dtype))
    for name, factor in factors.items():
        out[name] = (out[name] * factor).astype(out[name].dtype)
    return out
```

```python
from contextlib import ExitStack

import concourse.bass as bass
from concourse import mybir

P = 128
NODES = 6250
D = 256
EDGES = 106250
NT = -(-NODES // P)
NPAD = NT * P
ET = -(-EDGES // P)
EPAD = ET * P
KH = D // P
LAYERS = 4
EPS = 1e-5
DUMP = NPAD + 1

ALU = mybir.AluOpType
ACT = mybir.ActivationFunctionType
AX_X = mybir.AxisListType.X
F32 = mybir.dt.float32
I32 = mybir.dt.int32
U32 = mybir.dt.uint32


class Mem:

    def __init__(self, nc, ctx):
        self.nc, self.ctx = nc, ctx

    def sb(self, name, shape, dt=F32):
        return self.ctx.enter_context(self.nc.sbuf_tensor(name, shape, dt))

    def ps(self, name, shape, dt=F32):
        return self.ctx.enter_context(self.nc.psum_tensor(name, shape, dt))

    def sem(self, name):
        return self.ctx.enter_context(self.nc.semaphore(name))


def build_general(nc, x, src, dst, weights, vectors, out):
    h_dram = [nc.dram_tensor(f"g_h{i}", (NPAD, D), F32, kind="Internal").ap() for i in range(LAYERS)]
    agg_dram = nc.dram_tensor("g_agg", (NPAD, D + 1), F32, kind="Internal").ap()

    with ExitStack() as ctx:
        mem = Mem(nc, ctx)
        ident = mem.sb("g_ident", [P, P])
        earlier = mem.sb("g_earlier", [P, P])
        w = mem.sb("g_w", [P, LAYERS, 2, KH, D])
        vec = mem.sb("g_vec", [P, 6, D])
        zero = mem.sb("g_zero", [P, D + 1])
        src_idx = mem.sb("g_src_idx", [P, 1], I32)
        dst_idx = mem.sb("g_dst_idx", [P, 1], I32)
        put_idx = mem.sb("g_put_idx", [P, 1], I32)
        dst_f = mem.sb("g_dst_f", [P, 1])
        dst_wide = mem.sb("g_dst_wide", [P, P])
        same = mem.sb("g_same", [P, P])
        before = mem.sb("g_before", [P, P])
        repeats = mem.sb("g_repeats", [P, 1])
        put_f = mem.sb("g_put_f", [P, 1])
        msg = mem.sb("g_msg", [P, D + 1])
        old = mem.sb("g_old", [P, D + 1])
        new = mem.sb("g_new", [P, D + 1])
        h_t = mem.sb("g_h_t", [P, D])
        agg_t = mem.sb("g_agg_t", [P, D + 1])
        res_t = mem.sb("g_res_t", [P, D])
        mean_t = mem.sb("g_mean_t", [P, D])
        turned = mem.sb("g_turned", [P, 2, KH, P])
        y = mem.sb("g_y", [P, D])
        z = mem.sb("g_z", [P, D])
        stats = mem.sb("g_stats", [P, 6])
        mv = mem.sb("g_mv", [P, 2])
        col = mem.sb("g_col", [P, 4])
        spare = mem.sb("g_spare", [P, 1])
        spare_pool = mem.sb("g_spare_pool", [P, 2])
        ps_dst = mem.ps("g_ps_dst", [P, P])
        ps_sum = mem.ps("g_ps_sum", [P, D + 1])
        ps_turn = mem.ps("g_ps_turn", [P, 2, KH, P])
        ps_out = mem.ps("g_ps_out", [P, D])

        loaded = mem.sem("g_loaded")
        ready = mem.sem("g_ready")
        made = mem.sem("g_made")
        paced = mem.sem("g_paced")
        cleared = mem.sem("g_cleared")
        idx_in = mem.sem("g_idx_in")
        msg_in = mem.sem("g_msg_in")
        old_in = mem.sem("g_old_in")
        put_out = mem.sem("g_put_out")
        turned_dst = mem.sem("g_turned_dst")
        summed = mem.sem("g_summed")
        v = mem.sem("g_v")
        node_in = mem.sem("g_node_in")
        node_out = mem.sem("g_node_out")
        turn_done = mem.sem("g_turn_done")
        proj_done = mem.sem("g_proj_done")
        root = mem.sem("g_root")
        block = ctx.enter_context(nc.Block())

        EDGE_STEPS = 8
        PREP_STEPS = 8
        NODE_STEPS = [11, 4, 4, 11]

        def v_at_edges(layer):
            return 1 + NT * PREP_STEPS + sum(ET * EDGE_STEPS + NT * s for s in NODE_STEPS[:layer])

        def v_at_nodes(layer):
            return v_at_edges(layer) + ET * EDGE_STEPS

        def rows(dram, i):
            return dram[bass.ts(i, P), :]

        @block.gpsimd
        def _(pool):
            pool.dma_start(w[:], weights).then_inc(loaded, 16)
            pool.dma_start(vec[:], vectors).then_inc(loaded, 16)
            nc.gpsimd.memset(ident[:], 0.0).then_inc(made, 1)
            nc.gpsimd.memset(earlier[:], 1.0).then_inc(made, 1)
            pool.wait_ge(made, 2)
            nc.gpsimd.affine_select(out=ident[:], in_=ident[:], compare_op=ALU.not_equal, fill=1.0, base=0,
                                    pattern=[[-1, P]], channel_multiplier=1).then_inc(ready, 1)
            nc.gpsimd.affine_select(out=earlier[:], in_=earlier[:], compare_op=ALU.is_gt, fill=0.0, base=0,
                                    pattern=[[-1, P]], channel_multiplier=1).then_inc(ready, 1)
            def pace():
                nc.gpsimd.tensor_tensor(spare_pool[:, 0:1], spare_pool[:, 1:2], spare_pool[:, 1:2],
                                        ALU.add).then_inc(paced, 1)

            nc.gpsimd.memset(spare_pool[:], 0.0).then_inc(paced, 1)
            for layer in range(LAYERS):
                first = ET * layer
                pool.wait_ge(cleared, 16 * NT * (layer + 1))
                pool.wait_ge(node_out, 16 * NT * (layer + 1))
                with pool.Fori(0, ET) as t:
                    pool.wait_ge(ready, 2)
                    pool.wait_ge(paced, 2 * (t + first) + 1)
                    pool.wait_ge(idx_in, 32 * (t + first) + 32)
                    pace()
                    pool.indirect_dma_start(
                        out=msg[:, 0:D], out_offset=None, in_=h_dram[layer],
                        in_offset=bass.IndirectOffsetOnAxis(ap=src_idx[:].bitcast(U32), axis=0),
                        bounds_check=NPAD - 1, oob_is_err=False).then_inc(msg_in, 16)
                    pool.indirect_dma_start(
                        out=old[:], out_offset=None, in_=agg_dram,
                        in_offset=bass.IndirectOffsetOnAxis(ap=dst_idx[:].bitcast(U32), axis=0),
                        bounds_check=NPAD - 1, oob_is_err=False).then_inc(old_in, 16)
                    pool.wait_ge(ready, 2)
                    pool.wait_ge(paced, 2 * (t + first) + 2)
                    pool.wait_ge(v, t * EDGE_STEPS + v_at_edges(layer) + EDGE_STEPS)
                    pace()
                    pool.indirect_dma_start(
                        out=agg_dram, out_offset=bass.IndirectOffsetOnAxis(ap=put_idx[:].bitcast(U32), axis=0),
                        in_=new[:], in_offset=None,
                        bounds_check=NPAD - 1, oob_is_err=False).then_inc(put_out, 16)

        @block.sync
        def _(sp):
            with sp.Fori(0, NT) as i:
                sp.wait_ge(node_out, 16 * i)
                sp.dma_start(h_t[:], rows(x, i)).then_inc(node_in, 16)
                sp.wait_ge(v, i * PREP_STEPS + 1 + PREP_STEPS)
                sp.dma_start(rows(h_dram[0], i), y[:]).then_inc(node_out, 16)
            for layer in range(LAYERS):
                res = {0: x, 3: h_dram[1]}.get(layer)
                target = h_dram[layer + 1] if layer < LAYERS - 1 else out
                n_in = 3 if res is not None else 2
                sp.wait_ge(v, 1)
                sp.wait_ge(node_out, 16 * NT * (layer + 1))
                with sp.Fori(0, NT) as i:
                    sp.dma_start(rows(agg_dram, i), zero[:]).then_inc(cleared, 16)
                with sp.Fori(0, ET) as t:
                    sp.wait_ge(put_out, 16 * (t + ET * layer))
                    sp.dma_start(src_idx[:], src[bass.ts(t, P), :]).then_inc(idx_in, 16)
                    sp.dma_start(dst_idx[:], dst[bass.ts(t, P), :]).then_inc(idx_in, 16)
                sp.wait_ge(put_out, 16 * ET * (layer + 1))
                with sp.Fori(0, NT) as i:
                    sp.wait_ge(node_out, 16 * i + 16 * NT * (layer + 1))
                    sp.dma_start(agg_t[:], rows(agg_dram, i)).then_inc(node_in, 16)
                    sp.dma_start(h_t[:], rows(h_dram[layer], i)).then_inc(node_in, 16)
                    if res is not None:
                        sp.dma_start(res_t[:], rows(res, i)).then_inc(node_in, 16)
                    sp.wait_ge(v, i * NODE_STEPS[layer] + v_at_nodes(layer) + NODE_STEPS[layer])
                    sp.dma_start(rows(target, i), y[:]).then_inc(node_out, 16)
            sp.wait_ge(node_out, 16 * NT * (LAYERS + 1))

        @block.scalar
        def _(act):
            with act.Fori(0, NT) as i:
                act.wait_ge(v, i * PREP_STEPS + 1 + 3)
                nc.scalar.activation(col[:, 1:2], col[:, 0:1], ACT.Sqrt).then_inc(root, 1)
            for layer in (0, 3):
                with act.Fori(0, NT) as i:
                    act.wait_ge(v, i * NODE_STEPS[layer] + v_at_nodes(layer) + 8)
                    nc.scalar.activation(col[:, 1:2], col[:, 0:1], ACT.Sqrt).then_inc(root, 1)

        @block.vector
        def _(dve):
            def norm(source, at, roots):
                nc.vector.bn_stats(stats[:], source).then_inc(v, 1)
                dve.wait_ge(v, at + 1)
                nc.vector.memset(spare[:], 0.0)
                nc.vector.bn_aggr(mv[:], stats[:]).then_inc(v, 1)
                dve.wait_ge(v, at + 2)
                nc.vector.tensor_scalar_add(col[:, 0:1], mv[:, 1:2], EPS).then_inc(v, 1)
                dve.wait_ge(root, roots)
                nc.vector.reciprocal(col[:, 2:3], col[:, 1:2]).then_inc(v, 1)
                dve.wait_ge(v, at + 4)
                return nc.vector.tensor_scalar(z[:] if source is not y[:] else y[:], source, mv[:, 0:1],
                                               col[:, 2:3], ALU.subtract, ALU.mult)

            nc.vector.memset(msg[:, D:D + 1], 1.0)
            nc.vector.memset(zero[:], 0.0).then_inc(v, 1)
            dve.wait_ge(loaded, 32)
            with dve.Fori(0, NT) as i:
                at = i * PREP_STEPS + 1
                dve.wait_ge(node_in, 16 * i + 16)
                norm(h_t[:], at, i + 1).then_inc(v, 1)
                dve.wait_ge(v, at + 5)
                nc.vector.tensor_tensor(z[:], z[:], vec[:, 4, :], ALU.mult).then_inc(v, 1)
                dve.wait_ge(v, at + 6)
                nc.vector.tensor_tensor(z[:], z[:], vec[:, 5, :], ALU.add).then_inc(v, 1)
                dve.wait_ge(v, at + 7)
                nc.vector.tensor_scalar_max(y[:], z[:], 0.0).then_inc(v, 1)
            loads, roots = NT, NT
            for layer in range(LAYERS):
                first = ET * layer
                with dve.Fori(0, ET) as t:
                    at = t * EDGE_STEPS + v_at_edges(layer)
                    dve.wait_ge(idx_in, 32 * (t + first) + 32)
                    nc.vector.tensor_copy(dst_f[:], dst_idx[:]).then_inc(v, 1)
                    dve.wait_ge(v, at + 1)
                    nc.vector.tensor_copy(dst_wide[:], dst_f[:].to_broadcast([P, P])).then_inc(v, 1)
                    dve.wait_ge(turned_dst, t + first + 1)
                    nc.vector.tensor_scalar(same[:], ps_dst[:], dst_f[:], None, ALU.is_equal).then_inc(v, 1)
                    dve.wait_ge(v, at + 3)
                    nc.vector.tensor_tensor(before[:], same[:], earlier[:], ALU.mult).then_inc(v, 1)
                    dve.wait_ge(v, at + 4)
                    nc.vector.tensor_reduce(repeats[:], before[:], AX_X, ALU.max).then_inc(v, 1)
                    dve.wait_ge(v, at + 5)
                    nc.vector.scalar_tensor_tensor(out=put_f[:], in0=repeats[:], scalar=float(DUMP), in1=dst_f[:],
                                                   op0=ALU.mult, op1=ALU.add).then_inc(v, 1)
                    dve.wait_ge(v, at + 6)
                    nc.vector.tensor_copy(put_idx[:], put_f[:]).then_inc(v, 1)
                    dve.wait_ge(summed, t + first + 1)
                    dve.wait_ge(old_in, 16 * (t + first) + 16)
                    nc.vector.tensor_tensor(new[:], ps_sum[:], old[:], ALU.add).then_inc(v, 1)
                n_in = 3 if layer in (0, 3) else 2
                with dve.Fori(0, NT) as i:
                    steps = NODE_STEPS[layer]
                    at = i * steps + v_at_nodes(layer)
                    dve.wait_ge(node_in, 16 * n_in * i + 16 * (loads + n_in))
                    nc.vector.tensor_scalar_max(col[:, 3:4], agg_t[:, D:D + 1], 1.0).then_inc(v, 1)
                    dve.wait_ge(v, at + 1)
                    nc.vector.reciprocal(col[:, 2:3], col[:, 3:4]).then_inc(v, 1)
                    dve.wait_ge(v, at + 2)
                    nc.vector.tensor_scalar_mul(mean_t[:], agg_t[:, 0:D], col[:, 2:3]).then_inc(v, 1)
                    dve.wait_ge(turn_done, i + NT * layer + 1)
                    nc.vector.tensor_copy(turned[:], ps_turn[:]).then_inc(ready, 1)
                    dve.wait_ge(proj_done, i + NT * layer + 1)
                    nc.vector.tensor_tensor(z[:], ps_out[:], vec[:, layer, :], ALU.add).then_inc(ready, 1)
                    dve.wait_ge(ready, 2 + i * 2 + 2 * NT * layer + 2)
                    if layer in (1, 2):
                        nc.vector.tensor_scalar_max(y[:], z[:], 0.0).then_inc(v, 1)
                    else:
                        nc.vector.tensor_tensor(y[:], z[:], res_t[:], ALU.add).then_inc(v, 1)
                        dve.wait_ge(v, at + 4)
                        nc.vector.tensor_copy(z[:], y[:]).then_inc(v, 1)
                        dve.wait_ge(v, at + 5)
                        nc.vector.bn_stats(stats[:], z[:]).then_inc(v, 1)
                        dve.wait_ge(v, at + 6)
                        nc.vector.memset(spare[:], 0.0)
                        nc.vector.bn_aggr(mv[:], stats[:]).then_inc(v, 1)
                        dve.wait_ge(v, at + 7)
                        nc.vector.tensor_scalar_add(col[:, 0:1], mv[:, 1:2], EPS).then_inc(v, 1)
                        dve.wait_ge(root, i + roots + 1)
                        nc.vector.reciprocal(col[:, 2:3], col[:, 1:2]).then_inc(v, 1)
                        dve.wait_ge(v, at + 9)
                        nc.vector.tensor_scalar(y[:], z[:], mv[:, 0:1], col[:, 2:3], ALU.subtract,
                                                ALU.mult).then_inc(v, 1)
                        dve.wait_ge(v, at + 10)
                        nc.vector.tensor_copy(z[:], y[:]).then_inc(v, 1)
                loads += n_in * NT
                if layer == 0:
                    roots += NT

        @block.tensor
        def _(pe):
            pe.wait_ge(ready, 2)
            pe.wait_ge(loaded, 32)
            for layer in range(LAYERS):
                first = ET * layer
                with pe.Fori(0, ET) as t:
                    at = t * EDGE_STEPS + v_at_edges(layer)
                    pe.wait_ge(v, at + 2)
                    nc.tensor.transpose(ps_dst[:], dst_wide[:], ident[:]).then_inc(turned_dst, 1)
                    pe.wait_ge(v, at + 3)
                    pe.wait_ge(msg_in, 16 * (t + first) + 16)
                    nc.tensor.matmul(ps_sum[:], same[:], msg[:], start=True, stop=True).then_inc(summed, 1)
                with pe.Fori(0, NT) as i:
                    pe.wait_ge(v, i * NODE_STEPS[layer] + v_at_nodes(layer) + 3)
                    for k in range(KH):
                        nc.tensor.transpose(ps_turn[:, 0, k, :], mean_t[:, k * P:(k + 1) * P], ident[:])
                        last = nc.tensor.transpose(ps_turn[:, 1, k, :], h_t[:, k * P:(k + 1) * P], ident[:])
                    last.then_inc(turn_done, 1)
                    pe.wait_ge(ready, 2 + i * 2 + 2 * NT * layer + 1)
                    for side in range(2):
                        for k in range(KH):
                            last = nc.tensor.matmul(ps_out[:], turned[:, side, k, :], w[:, layer, side, k, :],
                                                    start=(side == 0 and k == 0), stop=(side == 1 and k == KH - 1))
                    last.then_inc(proj_done, 1)


def kernel(**inputs):
    import numpy as np
    import concourse.bacc as bacc
    from concourse import mybir as mb
    from concourse.bass_utils import run_bass_kernel_spmd as run

    def pad_rows(a, rows, fill):
        a = np.asarray(a)
        return np.concatenate([a, np.full((rows - a.shape[0],) + a.shape[1:], fill, a.dtype)])

    sides = [("L0_gnn_W_l", "L0_gnn_W_r")] + [(f"L1_gnn_W{i}l", f"L1_gnn_W{i}r") for i in (1, 2, 3)]
    w = np.stack([np.stack([np.asarray(inputs[n]).T.reshape(KH, P, D) for n in s]) for s in sides])
    w = np.ascontiguousarray(w.transpose(3, 0, 1, 2, 4))
    vec = np.stack([np.asarray(inputs[n]) for n in
                    ("L0_gnn_b_l", "L1_gnn_b1l", "L1_gnn_b2l", "L1_gnn_b3l", "L0_gnn_gamma", "L0_gnn_beta")])
    arrays = {
        "x": pad_rows(inputs["x"], NPAD, 0),
        "src": pad_rows(inputs["src"], EPAD, 0).reshape(EPAD, 1),
        "dst": pad_rows(inputs["dst"], EPAD, NPAD - 1).reshape(EPAD, 1),
        "weights": w,
        "vectors": np.ascontiguousarray(np.broadcast_to(vec, (P,) + vec.shape)),
    }
    nc = bacc.Bacc("TRN2", target_bir_lowering=False, num_devices=1)
    args = [nc.dram_tensor(f"in_{n}_dram", a.shape, mb.dt.from_np(a.dtype), kind="ExternalInput").ap()
            for n, a in arrays.items()]
    out = nc.dram_tensor("out_0_dram", (NPAD, D), F32, kind="ExternalOutput").ap()
    build_general(nc, *args, out)
    r = run(nc, [{f"in_{n}_dram": a for n, a in arrays.items()}], core_ids=[0])
    return r.results[0]["out_0_dram"][:NODES]
```

```python
from contextlib import ExitStack

import concourse.bass as bass
from concourse import mybir

P = 128
NODES = 6250
D = 256
EDGES = 106250
NT = -(-NODES // P)
NPAD = NT * P
ET = -(-EDGES // P)
EPAD = ET * P
KH = D // P
LAYERS = 4
EPS = 1e-5
DUMP = NPAD + 1
SW = 256
NS = -(-NPAD // SW)
GD = 4
NG = NPAD // GD
NGS = NS * SW // GD
SG = SW // GD
GP = 112
GC = NG // GP
KW = GD * NT
PT = 7
HOTS = 4
assert GP * GC == NG and NT % PT == 0 and NS * SW == NPAD + P and NT % 2 == 1 and 2 * KW <= 512

ALU = mybir.AluOpType
ACT = mybir.ActivationFunctionType
AX_X = mybir.AxisListType.X
F16 = mybir.dt.float16
F32 = mybir.dt.float32
I32 = mybir.dt.int32
U32 = mybir.dt.uint32


class Mem:

    def __init__(self, nc, ctx):
        self.nc, self.ctx = nc, ctx

    def sb(self, name, shape, dt=F32):
        return self.ctx.enter_context(self.nc.sbuf_tensor(name, shape, dt))

    def ps(self, name, shape, dt=F32):
        return self.ctx.enter_context(self.nc.psum_tensor(name, shape, dt))

    def sem(self, name):
        return self.ctx.enter_context(self.nc.semaphore(name))


class Shared:

    def __init__(self, mem):
        self.ident = mem.sb("ident", [P, P])
        self.ident16 = mem.sb("ident16", [P, P], F16)
        self.ones = mem.sb("ones", [P, P])
        self.eps = mem.sb("eps", [P, 1])
        self.iota = mem.sb("iota", [P, KW], F16)
        self.w = mem.sb("w", [P, LAYERS, 2, KH, D])
        self.vec = mem.sb("vec", [P, 6, D])
        self.key_t = mem.sb("key_t", [P, NGS])
        self.lo_t = mem.sb("lo_t", [P, NGS])
        self.deg = mem.sb("deg", [GP, GC, GD])
        self.dense = mem.sb("dense", [1, 1], I32)


def find_windows(nc, mem, sh, heads, edges, dst_rows, weights, vectors):
    heads_i = mem.sb("w_heads_i", [GP, ET], I32)
    heads_f = mem.sb("w_heads_f", [GP, ET])
    below = mem.sb("w_below", [GP, 2, ET])
    first_dst = mem.sb("w_first_dst", [GP, GC])
    row_f = mem.sb("w_row_f", [GP, GC])
    row_i = mem.sb("w_row_i", [GP, GC], I32)
    row_dst = mem.sb("w_row_dst", [GP, GC, P], I32)
    in_row = mem.sb("w_in_row", [GP, GC])
    start_f = mem.sb("w_start_f", [GP, GC])
    start_i = mem.sb("w_start_i", [GP, GC], I32)
    window = mem.sb("w_window", [GP, GC, 2 * P], I32)
    rel = mem.sb("w_rel", [GP, GC, P])
    bits = mem.sb("w_bits", [GP, GC, P], I32)
    low_bits = mem.sb("w_low_bits", [GP, GC, P], I32)
    lo = mem.sb("w_lo", [GP, GC, P])
    key = mem.sb("w_key", [GP, GC, P])
    total = mem.sb("w_total", [GP, 1])
    ps_t = [mem.ps(f"w_ps{i}", [P, 512]) for i in range(8)]

    made = mem.sem("w_made")
    heads_in = mem.sem("w_heads_in")
    params_in = mem.sem("w_params_in")
    v = mem.sem("w_v")
    compared = mem.sem("w_compared")
    ranked = mem.sem("w_ranked")
    rows_ready = mem.sem("w_rows_ready")
    rows_in = mem.sem("w_rows_in")
    starts_ready = mem.sem("w_starts_ready")
    windows_in = mem.sem("w_windows_in")
    lo_ready = mem.sem("w_lo_ready")
    key_ready = mem.sem("w_key_ready")
    lo_turned = mem.sem("w_lo_turned")
    key_turned = mem.sem("w_key_turned")
    total_ready = mem.sem("w_total_ready")
    total_done = mem.sem("w_total_done")
    copied = mem.sem("w_copied")
    PER = 4
    BANKS = -(-GC // PER)

    def wide(columns):
        return columns[:].unsqueeze(2).to_broadcast([GP, GC, P])

    with nc.Block() as block:
        @block.sync
        def _(sp):
            sp.dma_start(heads_i[:], heads).then_inc(heads_in, 16)
            sp.dma_start(sh.w[:].rearrange("p l s k d -> p (l s k d)"),
                         weights.rearrange("p l s k d -> p (l s k d)")).then_inc(params_in, 16)
            sp.dma_start(sh.vec[:].rearrange("p v d -> p (v d)"),
                         vectors.rearrange("p v d -> p (v d)")).then_inc(params_in, 16)
            sp.wait_ge(params_in, 32)

        @block.gpsimd
        def _(pool):
            nc.gpsimd.iota(first_dst[:], pattern=[[GD * GP, GC]], base=0, channel_multiplier=GD,
                           allow_small_or_imprecise_dtypes=True).then_inc(made, 1)
            nc.gpsimd.memset(sh.ident[:], 0.0).then_inc(made, 1)
            nc.gpsimd.iota(sh.iota[:], pattern=[[1, KW]], base=0, channel_multiplier=0,
                           allow_small_or_imprecise_dtypes=True).then_inc(made, 1)
            nc.gpsimd.memset(sh.ones[:], 1.0).then_inc(made, 1)
            nc.gpsimd.memset(sh.eps[:], EPS).then_inc(made, 1)
            nc.gpsimd.memset(sh.key_t[:, NG:NGS], -1.0).then_inc(made, 1)
            nc.gpsimd.memset(sh.lo_t[:, NG:NGS], 0.0).then_inc(made, 1)
            pool.wait_ge(made, 7)
            nc.gpsimd.affine_select(out=sh.ident[:], in_=sh.ident[:], compare_op=ALU.not_equal, fill=1.0, base=0,
                                    pattern=[[-1, P]], channel_multiplier=1).then_inc(made, 1)
            pool.wait_ge(made, 8)
            nc.gpsimd.tensor_copy(sh.ident16[:], sh.ident[:]).then_inc(made, 1)
            pool.wait_ge(rows_ready, 1)
            for c in range(GC):
                pool.indirect_dma_start(
                    out=row_dst[:, c, :], out_offset=None, in_=dst_rows,
                    in_offset=bass.IndirectOffsetOnAxis(ap=row_i[:, c:c + 1].bitcast(U32), axis=0)
                ).then_inc(rows_in, 16)
            pool.wait_ge(starts_ready, 1)
            for c in range(GC):
                pool.indirect_dma_start(
                    out=window[:, c, :], out_offset=None, in_=edges.rearrange("n (t o) -> (n t) o", o=1),
                    in_offset=bass.IndirectOffsetOnAxis(ap=start_i[:, c:c + 1].bitcast(U32), axis=0)
                ).then_inc(windows_in, 16)

        @block.scalar
        def _(act):
            for c in range(GC):
                act.wait_ge(compared, c + 1)
                nc.scalar.activation(below[:, c % 2, :], below[:, c % 2, :], ACT.Copy,
                                     accum_out=row_f[:, c:c + 1]).then_inc(ranked, 1)
            for source, bank0, target in ((lo_turned, 0, sh.lo_t), (key_turned, BANKS, sh.key_t)):
                for i in range(BANKS):
                    n = min(PER, GC - i * PER) * GP
                    act.wait_ge(source, i + 1)
                    nc.scalar.activation(target[:, i * PER * GP:i * PER * GP + n], ps_t[bank0 + i][:, 0:n],
                                         ACT.Copy).then_inc(copied, 1)

        @block.tensor
        def _(pe):
            pe.wait_ge(made, 9)
            for ready_sem, source, bank0, done in ((lo_ready, lo, 0, lo_turned), (key_ready, key, BANKS, key_turned)):
                pe.wait_ge(ready_sem, 1)
                for i in range(BANKS):
                    for j in range(min(PER, GC - i * PER)):
                        last = nc.tensor.transpose(ps_t[bank0 + i][:, j * GP:(j + 1) * GP],
                                                   source[:, i * PER + j, :], sh.ident[0:GP, 0:GP])
                    last.then_inc(done, 1)
            pe.wait_ge(total_ready, 1)
            pe.wait_ge(copied, 1)
            nc.tensor.matmul(ps_t[0][0:1, 0:1], total[:], sh.ones[0:GP, 0:1], start=True, stop=True).then_inc(total_done, 1)

        @block.vector
        def _(dve):
            steps = [0]

            def link(ins):
                steps[0] += 1
                ins.then_inc(v, 1)
                dve.wait_ge(v, steps[0])

            dve.wait_ge(heads_in, 16)
            link(nc.vector.tensor_copy(heads_f[:], heads_i[:]))
            dve.wait_ge(made, 1)
            for c in range(GC):
                if c >= 2:
                    dve.wait_ge(ranked, c - 1)
                nc.vector.tensor_scalar(below[:, c % 2, :], heads_f[:], first_dst[:, c:c + 1], None,
                                        ALU.is_lt).then_inc(compared, 1)
            dve.wait_ge(ranked, GC)
            link(nc.vector.tensor_scalar(row_f[:], row_f[:], -1.0, 0.0, ALU.add, ALU.max))
            nc.vector.tensor_copy(row_i[:], row_f[:]).then_inc(rows_ready, 1)
            dve.wait_ge(rows_in, 16 * GC)
            link(nc.vector.tensor_tensor(rel[:], row_dst[:], wide(first_dst), ALU.is_lt))
            link(nc.vector.tensor_reduce(in_row[:], rel[:], AX_X, ALU.add))
            link(nc.vector.scalar_tensor_tensor(out=start_f[:], in0=row_f[:], scalar=float(P), in1=in_row[:],
                                                op0=ALU.mult, op1=ALU.add))
            link(nc.vector.tensor_scalar(start_f[:], start_f[:], float(EPAD - P), 2.0, ALU.min, ALU.mult))
            nc.vector.tensor_copy(start_i[:], start_f[:]).then_inc(starts_ready, 1)
            dve.wait_ge(windows_in, 16 * GC)
            pairs = window[:].rearrange("p c (e t) -> p c e t", t=2)
            link(nc.vector.tensor_scalar(low_bits[:], pairs[:, :, :, 0], P - 1, None, ALU.bitwise_and))
            nc.vector.tensor_copy(lo[:], low_bits[:]).then_inc(lo_ready, 1)
            nc.vector.tensor_scalar(bits[:], pairs[:, :, :, 0], 7, None, ALU.logical_shift_right).then_inc(v, 1)
            steps[0] += 1
            link(nc.vector.tensor_tensor(rel[:], pairs[:, :, :, 1], wide(first_dst), ALU.subtract))
            nc.vector.scalar_tensor_tensor(out=key[:], in0=rel[:], scalar=float(NT), in1=bits[:], op0=ALU.mult,
                                           op1=ALU.add).then_inc(key_ready, 1)
            for j in range(GD):
                link(nc.vector.tensor_scalar(row_dst[:].bitcast(F32), rel[:], float(j), None, ALU.is_equal))
                link(nc.vector.tensor_reduce(sh.deg[:, :, j], row_dst[:].bitcast(F32), AX_X, ALU.add))
            nc.vector.tensor_reduce(total[:], sh.deg[:].rearrange("p c j -> p (c j)"), AX_X,
                                    ALU.add).then_inc(total_ready, 1)
            dve.wait_ge(total_done, 1)
            link(nc.vector.tensor_scalar(sh.dense[:], ps_t[0][0:1, 0:1], float(EPAD), None, ALU.is_equal))


def general(nc, mem, shared, x, edges, out):
    ident, w, vec = shared.ident, shared.w, shared.vec
    h_dram = [nc.dram_tensor(f"g_h{i}", (NPAD, D), F32, kind="Internal").ap() for i in range(LAYERS)]
    agg_dram = nc.dram_tensor("g_agg", (NPAD, D + 1), F32, kind="Internal").ap()
    earlier = mem.sb("g_earlier", [P, P])
    zero = mem.sb("g_zero", [P, D + 1])
    pair = mem.sb("g_pair", [P, 2], I32)
    put_idx = mem.sb("g_put_idx", [P, 1], I32)
    dst_f = mem.sb("g_dst_f", [P, 1])
    dst_wide = mem.sb("g_dst_wide", [P, P])
    same = mem.sb("g_same", [P, P])
    before = mem.sb("g_before", [P, P])
    repeats = mem.sb("g_repeats", [P, 1])
    put_f = mem.sb("g_put_f", [P, 1])
    msg = mem.sb("g_msg", [P, D + 1])
    old = mem.sb("g_old", [P, D + 1])
    new = mem.sb("g_new", [P, D + 1])
    h_t = mem.sb("g_h_t", [P, D])
    agg_t = mem.sb("g_agg_t", [P, D + 1])
    res_t = mem.sb("g_res_t", [P, D])
    mean_t = mem.sb("g_mean_t", [P, D])
    turned = mem.sb("g_turned", [P, 2, KH, P])
    y = mem.sb("g_y", [P, D])
    z = mem.sb("g_z", [P, D])
    stats = mem.sb("g_stats", [P, 6])
    mv = mem.sb("g_mv", [P, 2])
    col = mem.sb("g_col", [P, 4])
    spare = mem.sb("g_spare", [P, 1])
    spare_pool = mem.sb("g_spare_pool", [P, 2])
    ps_dst = mem.ps("g_ps_dst", [P, P])
    ps_sum = mem.ps("g_ps_sum", [P, D + 1])
    ps_turn = mem.ps("g_ps_turn", [P, 2, KH, P])
    ps_out = mem.ps("g_ps_out", [P, D])

    ready = mem.sem("g_ready")
    made = mem.sem("g_made")
    paced = mem.sem("g_paced")
    cleared = mem.sem("g_cleared")
    idx_in = mem.sem("g_idx_in")
    msg_in = mem.sem("g_msg_in")
    old_in = mem.sem("g_old_in")
    put_out = mem.sem("g_put_out")
    turned_dst = mem.sem("g_turned_dst")
    summed = mem.sem("g_summed")
    v = mem.sem("g_v")
    node_in = mem.sem("g_node_in")
    node_out = mem.sem("g_node_out")
    turn_done = mem.sem("g_turn_done")
    proj_done = mem.sem("g_proj_done")
    root = mem.sem("g_root")

    EDGE_STEPS = 8
    PREP_STEPS = 8
    NODE_STEPS = [11, 4, 4, 11]

    def v_at_edges(layer):
        return 1 + NT * PREP_STEPS + sum(ET * EDGE_STEPS + NT * s for s in NODE_STEPS[:layer])

    def v_at_nodes(layer):
        return v_at_edges(layer) + ET * EDGE_STEPS

    def rows(dram, i):
        return dram[bass.ts(i, P), :]

    def gpsimd(pool):
        nc.gpsimd.memset(earlier[:], 1.0).then_inc(made, 1)
        pool.wait_ge(made, 1)
        nc.gpsimd.affine_select(out=earlier[:], in_=earlier[:], compare_op=ALU.is_gt, fill=0.0, base=0,
                                pattern=[[-1, P]], channel_multiplier=1).then_inc(ready, 1)
        def pace():
            nc.gpsimd.tensor_tensor(spare_pool[:, 0:1], spare_pool[:, 1:2], spare_pool[:, 1:2],
                                    ALU.add).then_inc(paced, 1)

        nc.gpsimd.memset(spare_pool[:], 0.0).then_inc(paced, 1)
        for layer in range(LAYERS):
            first = ET * layer
            pool.wait_ge(cleared, 16 * NT * (layer + 1))
            pool.wait_ge(node_out, 16 * NT * (layer + 1))
            with pool.Fori(0, ET) as t:
                pool.wait_ge(ready, 2)
                pool.wait_ge(paced, 2 * (t + first) + 1)
                pool.wait_ge(idx_in, 16 * (t + first) + 16)
                pace()
                pool.indirect_dma_start(
                    out=msg[:, 0:D], out_offset=None, in_=h_dram[layer],
                    in_offset=bass.IndirectOffsetOnAxis(ap=pair[:, 0:1].bitcast(U32), axis=0),
                    bounds_check=NPAD - 1, oob_is_err=False).then_inc(msg_in, 16)
                pool.indirect_dma_start(
                    out=old[:], out_offset=None, in_=agg_dram,
                    in_offset=bass.IndirectOffsetOnAxis(ap=pair[:, 1:2].bitcast(U32), axis=0),
                    bounds_check=NPAD - 1, oob_is_err=False).then_inc(old_in, 16)
                pool.wait_ge(ready, 2)
                pool.wait_ge(paced, 2 * (t + first) + 2)
                pool.wait_ge(v, t * EDGE_STEPS + v_at_edges(layer) + EDGE_STEPS)
                pace()
                pool.indirect_dma_start(
                    out=agg_dram, out_offset=bass.IndirectOffsetOnAxis(ap=put_idx[:].bitcast(U32), axis=0),
                    in_=new[:], in_offset=None,
                    bounds_check=NPAD - 1, oob_is_err=False).then_inc(put_out, 16)

    def sync(sp):
        sp.dma_start(h_t[:], rows(x, 0)).then_inc(node_in, 16)
        with sp.Fori(0, NT - 1) as i:
            sp.wait_ge(v, i * PREP_STEPS + 1 + PREP_STEPS)
            sp.dma_start(rows(h_dram[0], i), y[:]).then_inc(node_out, 16)
            sp.wait_ge(node_out, 16 * i + 16)
            sp.dma_start(h_t[:], rows(x, i + 1)).then_inc(node_in, 16)
        sp.wait_ge(v, NT * PREP_STEPS + 1)
        sp.dma_start(rows(h_dram[0], NT - 1), y[:]).then_inc(node_out, 16)
        for layer in range(LAYERS):
            res = {0: x, 3: h_dram[1]}.get(layer)
            target = h_dram[layer + 1] if layer < LAYERS - 1 else out
            n_in = 3 if res is not None else 2
            sp.wait_ge(v, 1)
            sp.wait_ge(node_out, 16 * NT * (layer + 1))
            with sp.Fori(0, NT) as i:
                sp.dma_start(rows(agg_dram, i), zero[:]).then_inc(cleared, 16)
            sp.dma_start(pair[:], edges[0:P, :]).then_inc(idx_in, 16)
            with sp.Fori(1, ET) as t:
                sp.wait_ge(put_out, 16 * (t + ET * layer))
                sp.dma_start(pair[:], edges[bass.ts(t, P), :]).then_inc(idx_in, 16)
            sp.wait_ge(put_out, 16 * ET * (layer + 1))
            with sp.Fori(0, NT) as i:
                sp.wait_ge(node_out, 16 * i + 16 * NT * (layer + 1))
                sp.dma_start(agg_t[:], rows(agg_dram, i)).then_inc(node_in, 16)
                sp.dma_start(h_t[:], rows(h_dram[layer], i)).then_inc(node_in, 16)
                if res is not None:
                    sp.dma_start(res_t[:], rows(res, i)).then_inc(node_in, 16)
                sp.wait_ge(v, i * NODE_STEPS[layer] + v_at_nodes(layer) + NODE_STEPS[layer])
                sp.dma_start(rows(target, i), y[:]).then_inc(node_out, 16)
        sp.wait_ge(node_out, 16 * NT * (LAYERS + 1))

    def scalar(act):
        with act.Fori(0, NT) as i:
            act.wait_ge(v, i * PREP_STEPS + 1 + 3)
            nc.scalar.activation(col[:, 1:2], col[:, 0:1], ACT.Sqrt).then_inc(root, 1)
        for layer in (0, 3):
            with act.Fori(0, NT) as i:
                act.wait_ge(v, i * NODE_STEPS[layer] + v_at_nodes(layer) + 8)
                nc.scalar.activation(col[:, 1:2], col[:, 0:1], ACT.Sqrt).then_inc(root, 1)

    def vector(dve):
        def norm(source, at, roots):
            nc.vector.bn_stats(stats[:], source).then_inc(v, 1)
            dve.wait_ge(v, at + 1)
            nc.vector.memset(spare[:], 0.0)
            nc.vector.bn_aggr(mv[:], stats[:]).then_inc(v, 1)
            dve.wait_ge(v, at + 2)
            nc.vector.tensor_scalar_add(col[:, 0:1], mv[:, 1:2], EPS).then_inc(v, 1)
            dve.wait_ge(root, roots)
            nc.vector.reciprocal(col[:, 2:3], col[:, 1:2]).then_inc(v, 1)
            dve.wait_ge(v, at + 4)
            return nc.vector.tensor_scalar(z[:] if source is not y[:] else y[:], source, mv[:, 0:1],
                                           col[:, 2:3], ALU.subtract, ALU.mult)

        nc.vector.memset(msg[:, D:D + 1], 1.0)
        nc.vector.memset(zero[:], 0.0).then_inc(v, 1)
        with dve.Fori(0, NT) as i:
            at = i * PREP_STEPS + 1
            dve.wait_ge(node_in, 16 * i + 16)
            norm(h_t[:], at, i + 1).then_inc(v, 1)
            dve.wait_ge(v, at + 5)
            nc.vector.tensor_tensor(z[:], z[:], vec[:, 4, :], ALU.mult).then_inc(v, 1)
            dve.wait_ge(v, at + 6)
            nc.vector.tensor_tensor(z[:], z[:], vec[:, 5, :], ALU.add).then_inc(v, 1)
            dve.wait_ge(v, at + 7)
            nc.vector.tensor_scalar_max(y[:], z[:], 0.0).then_inc(v, 1)
        loads, roots = NT, NT
        for layer in range(LAYERS):
            first = ET * layer
            with dve.Fori(0, ET) as t:
                at = t * EDGE_STEPS + v_at_edges(layer)
                dve.wait_ge(idx_in, 16 * (t + first) + 16)
                nc.vector.tensor_copy(dst_f[:], pair[:, 1:2]).then_inc(v, 1)
                dve.wait_ge(v, at + 1)
                nc.vector.tensor_copy(dst_wide[:], dst_f[:].to_broadcast([P, P])).then_inc(v, 1)
                dve.wait_ge(turned_dst, t + first + 1)
                nc.vector.tensor_scalar(same[:], ps_dst[:], dst_f[:], None, ALU.is_equal).then_inc(v, 1)
                dve.wait_ge(v, at + 3)
                nc.vector.tensor_tensor(before[:], same[:], earlier[:], ALU.mult).then_inc(v, 1)
                dve.wait_ge(v, at + 4)
                nc.vector.tensor_reduce(repeats[:], before[:], AX_X, ALU.max).then_inc(v, 1)
                dve.wait_ge(v, at + 5)
                nc.vector.scalar_tensor_tensor(out=put_f[:], in0=repeats[:], scalar=float(DUMP), in1=dst_f[:],
                                               op0=ALU.mult, op1=ALU.add).then_inc(v, 1)
                dve.wait_ge(v, at + 6)
                nc.vector.tensor_copy(put_idx[:], put_f[:]).then_inc(v, 1)
                dve.wait_ge(summed, t + first + 1)
                dve.wait_ge(old_in, 16 * (t + first) + 16)
                nc.vector.tensor_tensor(new[:], ps_sum[:], old[:], ALU.add).then_inc(v, 1)
            n_in = 3 if layer in (0, 3) else 2
            with dve.Fori(0, NT) as i:
                steps = NODE_STEPS[layer]
                at = i * steps + v_at_nodes(layer)
                dve.wait_ge(node_in, 16 * n_in * i + 16 * (loads + n_in))
                nc.vector.tensor_scalar_max(col[:, 3:4], agg_t[:, D:D + 1], 1.0).then_inc(v, 1)
                dve.wait_ge(v, at + 1)
                nc.vector.reciprocal(col[:, 2:3], col[:, 3:4]).then_inc(v, 1)
                dve.wait_ge(v, at + 2)
                nc.vector.tensor_scalar_mul(mean_t[:], agg_t[:, 0:D], col[:, 2:3]).then_inc(v, 1)
                dve.wait_ge(turn_done, i + NT * layer + 1)
                nc.vector.tensor_copy(turned[:], ps_turn[:]).then_inc(ready, 1)
                dve.wait_ge(proj_done, i + NT * layer + 1)
                nc.vector.tensor_tensor(z[:], ps_out[:], vec[:, layer, :], ALU.add).then_inc(ready, 1)
                dve.wait_ge(ready, 1 + i * 2 + 2 * NT * layer + 2)
                if layer in (1, 2):
                    nc.vector.tensor_scalar_max(y[:], z[:], 0.0).then_inc(v, 1)
                else:
                    nc.vector.tensor_tensor(y[:], z[:], res_t[:], ALU.add).then_inc(v, 1)
                    dve.wait_ge(v, at + 4)
                    nc.vector.tensor_copy(z[:], y[:]).then_inc(v, 1)
                    dve.wait_ge(v, at + 5)
                    nc.vector.bn_stats(stats[:], z[:]).then_inc(v, 1)
                    dve.wait_ge(v, at + 6)
                    nc.vector.memset(spare[:], 0.0)
                    nc.vector.bn_aggr(mv[:], stats[:]).then_inc(v, 1)
                    dve.wait_ge(v, at + 7)
                    nc.vector.tensor_scalar_add(col[:, 0:1], mv[:, 1:2], EPS).then_inc(v, 1)
                    dve.wait_ge(root, i + roots + 1)
                    nc.vector.reciprocal(col[:, 2:3], col[:, 1:2]).then_inc(v, 1)
                    dve.wait_ge(v, at + 9)
                    nc.vector.tensor_scalar(y[:], z[:], mv[:, 0:1], col[:, 2:3], ALU.subtract,
                                            ALU.mult).then_inc(v, 1)
                    dve.wait_ge(v, at + 10)
                    nc.vector.tensor_copy(z[:], y[:]).then_inc(v, 1)
            loads += n_in * NT
            if layer == 0:
                roots += NT

    def tensor(pe):
        pe.wait_ge(ready, 1)
        for layer in range(LAYERS):
            first = ET * layer
            with pe.Fori(0, ET) as t:
                at = t * EDGE_STEPS + v_at_edges(layer)
                pe.wait_ge(v, at + 2)
                nc.tensor.transpose(ps_dst[:], dst_wide[:], ident[:]).then_inc(turned_dst, 1)
                pe.wait_ge(v, at + 3)
                pe.wait_ge(msg_in, 16 * (t + first) + 16)
                nc.tensor.matmul(ps_sum[:], same[:], msg[:], start=True, stop=True).then_inc(summed, 1)
            with pe.Fori(0, NT) as i:
                pe.wait_ge(v, i * NODE_STEPS[layer] + v_at_nodes(layer) + 3)
                for k in range(KH):
                    nc.tensor.transpose(ps_turn[:, 0, k, :], mean_t[:, k * P:(k + 1) * P], ident[:])
                    last = nc.tensor.transpose(ps_turn[:, 1, k, :], h_t[:, k * P:(k + 1) * P], ident[:])
                last.then_inc(turn_done, 1)
                pe.wait_ge(ready, 1 + i * 2 + 2 * NT * layer + 1)
                for side in range(2):
                    for k in range(KH):
                        last = nc.tensor.matmul(ps_out[:], turned[:, side, k, :], w[:, layer, side, k, :],
                                                start=(side == 0 and k == 0), stop=(side == 1 and k == KH - 1))
                last.then_inc(proj_done, 1)

    return {"gpsimd": gpsimd, "sync": sync, "scalar": scalar, "vector": vector, "tensor": tensor}


class Strip:

    def __init__(self, layer, half, odd):
        self.layer, self.half, self.odd = layer, half, odd
        self.s = 2 * half + odd
        self.q = layer * NS + self.s
        self.slot = (layer * NS + odd) % 2
        self.tiles = layer * NT + (SW // P) * self.s

    def is_strip(self, s):
        return isinstance(self.s, int) and self.s == s

    @property
    def count(self):
        return 1 if self.is_strip(NS - 1) else SW // P

    def next(self):
        return Strip(self.layer, self.half + self.odd, 1 - self.odd)

    def before(self):
        if self.is_strip(0):
            return Strip(self.layer - 1, (NS - 1) // 2, 0) if self.layer else None
        return Strip(self.layer, self.half + self.odd - 1, 1 - self.odd)

    def uses(self, offset):
        return self.half + (offset + self.odd) // 2


def for_strips(eng, layer, body):
    body(Strip(layer, 0, 0))
    body(Strip(layer, 0, 1))
    with eng.Fori(0, (NS - 3) // 2) as k:
        body(Strip(layer, k + 1, 0))
        body(Strip(layer, k + 1, 1))
    body(Strip(layer, (NS - 1) // 2, 0))


def wait(eng, sem, value):
    if isinstance(value, int) and value <= 0:
        return
    eng.wait_ge(sem, value)


def groups_at(h):
    return range(SG * h // NT, SG * (h + 1) // NT)


TURN_AT, ROOT_AT, PROJECT_AT, Y_AT, SQRT_AT, Z_AT, APART = 4, 6, 14, 17, 18, 20, 20
NORM_LAYERS = {0: 0, LAYERS - 1: 1}


class Fast:

    def __init__(self, nc, mem, shared, x, out):
        self.nc, self.mem, self.x, self.out = nc, mem, x, out
        self.sh = shared
        self.a_dram = nc.dram_tensor("f_a_dram", (NS, P, NT * SW), F16, kind="Internal").ap()
        self.x1_dram = nc.dram_tensor("f_x1_dram", (NPAD, D), F32, kind="Internal").ap()
        self.deg_dram = nc.dram_tensor("f_deg_dram", (NPAD,), F32, kind="Internal").ap()
        sb, ps, sem = mem.sb, mem.ps, mem.sem
        self.hp = sb("f_hp", [P, 2, NT, 2, D], F16)
        self.a_sb = sb("f_a", [P, 2, NT, SW], F16)
        self.hot_key = sb("f_hot_key", [P, HOTS, KW], F16)
        self.hot_lo = sb("f_hot_lo", [P, HOTS, P], F16)
        self.sums_t = sb("f_sums_t", [P, KH, SW])
        self.root_t = sb("f_root_t", [P, 2, KH, P])
        self.y = sb("f_y", [P, 2, D])
        self.z = sb("f_z", [P, 2, D])
        self.res = sb("f_res", [P, 2, D])
        self.stats = sb("f_stats", [P, PT, 6])
        self.mv = sb("f_mv", [P, PT, 2])
        self.dev = sb("f_dev", [P, PT])
        self.rstd = sb("f_rstd", [P, PT])
        self.carry = sb("f_carry", [P, 1])
        self.deg_n = sb("f_deg_n", [P, NT])
        self.rdeg = sb("f_rdeg", [P, NT])
        self.c_sum = sb("f_c_sum", [P, LAYERS, NT])
        self.c_root = sb("f_c_root", [P, LAYERS])
        self.scale = sb("f_scale", [P, LAYERS])
        self.unscale = sb("f_unscale", [P, LAYERS])
        self.after = sb("f_after", [P, LAYERS])
        self.bound = sb("f_bound", [P, LAYERS])
        self.vec_max = sb("f_vec_max", [P, 6])
        self.row_max = sb("f_row_max", [P, 2])
        work = self.hp[:, 1].rearrange("p t c d -> p (t c d)").bitcast(F32)
        n = PT * D
        self.x_tiles = [work[:, b * n:(b + 1) * n].rearrange("p (t d) -> p t d", t=PT) for b in range(2)]
        self.x_norm = [work[:, (2 + b) * n:(3 + b) * n].rearrange("p (t d) -> p t d", t=PT) for b in range(2)]
        self.w_abs = work[:, 4 * n:4 * n + 8 * D]
        self.vec_abs = work[:, 4 * n + 8 * D:4 * n + 14 * D]

        self.ps_agg = [ps(f"f_ps_agg{b}", [P, KH, 512]) for b in range(2)]
        self.ps_build = [ps(f"f_ps_build{b}", [P, 512]) for b in range(2)]
        self.ps_proj = ps("f_ps_proj", [P, 2, D])
        self.ps_root = ps("f_ps_root", [P, KH, P])

        self.x_in = [sem(f"f_x_in{b}") for b in range(2)]
        self.deg_out = sem("f_deg_out")
        self.deg_in = sem("f_deg_in")
        self.prep = sem("f_prep")
        self.abs_done = sem("f_abs_done")
        self.rows_done = sem("f_rows_done")
        self.x_var = sem("f_x_var")
        self.x_dev = sem("f_x_dev")
        self.x_scaled = sem("f_x_scaled")
        self.x_shifted = sem("f_x_shifted")
        self.x_read = sem("f_x_read")
        self.x_pieces = sem("f_x_pieces")
        self.hot_done = sem("f_hot_done")
        self.counted = sem("f_counted")
        self.a_built = sem("f_a_built")
        self.a_out = [sem(f"f_a_out{b}") for b in range(2)]
        self.a_in = [sem(f"f_a_in{b}") for b in range(2)]
        self.agg_done = sem("f_agg_done")
        self.agg_out = sem("f_agg_out")
        self.turned = sem("f_turned")
        self.root_out = sem("f_root_out")
        self.proj_done = sem("f_proj_done")
        self.y_part = sem("f_y_part")
        self.y_done = sem("f_y_done")
        self.res_in = [sem(f"f_res_in{b}") for b in range(2)]
        self.res_done = sem("f_res_done")
        self.stat_done = sem("f_stat_done")
        self.var_done = sem("f_var_done")
        self.dev_done = sem("f_dev_done")
        self.rstd_done = sem("f_rstd_done")
        self.z_done = sem("f_z_done")
        self.z_out = [sem(f"f_z_out{b}") for b in range(2)]
        self.hi_done = sem("f_hi_done")
        self.piece_done = sem("f_piece_done")

    def tensor(self, pe):
        nc, sh = self.nc, self.sh

        def count(strip, g):
            n = strip.s * SG + g
            if g % 2 == 0:
                wait(pe, self.a_built, strip.s * (SG // 2) + g // 2 - 1)
            pe.wait_ge(self.hot_done, 2 * n + 2)
            nc.tensor.matmul(self.ps_build[g // 2 % 2][:, (g % 2) * KW:(g % 2 + 1) * KW],
                             self.hot_lo[:, g % HOTS, :], self.hot_key[:, g % HOTS, :],
                             start=True, stop=True).then_inc(self.counted, 1)

        def turn(strip, u):
            i = (SW // P) * strip.s + u
            for k in range(KH):
                for part in range(2):
                    last = nc.tensor.matmul(self.ps_root[:, k, :],
                                            self.hp[:, strip.layer % 2, i, part, k * P:(k + 1) * P],
                                            sh.ident16[:], start=(part == 0), stop=(part == 1))
            last.then_inc(self.turned, 1)

        def project(strip, u):
            n = strip.tiles + u
            wait(pe, self.y_done, n)
            pe.wait_ge(self.agg_out, strip.q + 1)
            for k in range(KH):
                nc.tensor.matmul(self.ps_proj[:, 0, :], self.sums_t[:, k, u * P:(u + 1) * P],
                                 sh.w[:, strip.layer, 0, k, :], start=(k == 0), stop=(k == KH - 1))
            pe.wait_ge(self.root_out, n + 1)
            for k in range(KH):
                last = nc.tensor.matmul(self.ps_proj[:, 1, :], self.root_t[:, u, k, :],
                                        sh.w[:, strip.layer, 1, k, :], start=(k == 0), stop=(k == KH - 1))
            last.then_inc(self.proj_done, 1)

        def body(strip, dense=True):
            done = strip.before()
            layer, b = strip.layer, strip.slot
            width = P if strip.is_strip(NS - 1) else SW
            for h in range(NT):
                for u in range(done.count if done else 0):
                    if h == TURN_AT + APART * u:
                        wait(pe, self.root_out, done.tiles + u)
                if dense:
                    if h == 0:
                        wait(pe, self.agg_out, strip.q - 1)
                        if layer == 0:
                            pe.wait_ge(self.a_built, (SG // 2) * (strip.s + 1))
                        else:
                            pe.wait_ge(self.a_in[b], 16 * (strip.uses((layer - 1) * NS) + 1))
                    if strip.is_strip(0) and layer:
                        pe.wait_ge(self.piece_done, (layer - 1) * NT + h + 1)
                    elif strip.is_strip(0):
                        pe.wait_ge(self.x_pieces, h // PT + 1)
                    for k in range(KH):
                        for part in range(2):
                            last = nc.tensor.matmul(
                                self.ps_agg[b][:, k, 0:width], self.hp[:, layer % 2, h, part, k * P:(k + 1) * P],
                                self.a_sb[:, b, h, 0:width], start=(h == 0 and part == 0),
                                stop=(h == NT - 1 and part == 1))
                    if h == NT - 1:
                        last.then_inc(self.agg_done, 1)
                for u in range(done.count if done else 0):
                    if h == TURN_AT + APART * u:
                        turn(done, u)
                    if h == PROJECT_AT + APART * u:
                        project(done, u)
                if dense and layer == 0 and not strip.is_strip(NS - 1):
                    for g in groups_at(h):
                        count(strip.next(), g)

        pe.wait_ge(self.abs_done, 1)
        for j in range(8):
            last = nc.tensor.matmul(self.ps_proj[:, j // 4, :], sh.ones[:], self.w_abs[:, j * D:(j + 1) * D],
                                    start=(j % 4 == 0), stop=(j % 4 == 3))
        last.then_inc(self.rows_done, 1)
        for g in range(SG):
            count(Strip(0, 0, 0), g)
        for layer in range(LAYERS):
            for_strips(pe, layer, body)
        body(Strip(LAYERS, 0, 0), dense=False)

    def scalar(self, act):
        nc, sh = self.nc, self.sh

        def keep(strip, j):
            if j == 0:
                wait(act, self.agg_done, strip.s - 1)
                wait(act, self.a_out[strip.slot], 16 * strip.half)
            act.wait_ge(self.counted, strip.s * SG + 2 * j + 2)
            nc.scalar.activation(self.a_sb[:, strip.slot, :, 2 * GD * j:2 * GD * (j + 1)],
                                 self.ps_build[j % 2][:, 0:2 * KW].rearrange("p (d h) -> p h d", h=NT),
                                 ACT.Copy).then_inc(self.a_built, 1)

        def body(strip, dense=True):
            done = strip.before()
            for h in range(NT):
                if done and h == 0:
                    act.wait_ge(self.agg_done, done.q + 1)
                    wait(act, self.proj_done, done.tiles)
                    nc.scalar.activation(self.sums_t[:], self.ps_agg[done.slot][:, :, 0:SW],
                                         ACT.Copy).then_inc(self.agg_out, 1)
                for u in range(done.count if done else 0):
                    n = done.tiles + u
                    if h == ROOT_AT + APART * u:
                        act.wait_ge(self.turned, n + 1)
                        wait(act, self.proj_done, n)
                        nc.scalar.activation(self.root_t[:, u], self.ps_root[:], ACT.Copy).then_inc(self.root_out, 1)
                    if h == SQRT_AT + APART * u and done.layer in NORM_LAYERS:
                        m = n - done.layer * NT + NORM_LAYERS[done.layer] * NT
                        act.wait_ge(self.var_done, m + 1)
                        nc.scalar.activation(self.dev[:, 0:1], self.mv[:, 0, 1:2], ACT.Sqrt,
                                             bias=sh.eps[:]).then_inc(self.dev_done, 1)
                if dense and strip.layer == 0 and not strip.is_strip(NS - 1):
                    for g in groups_at(h):
                        if g % 2:
                            keep(strip.next(), g // 2)

        for it in range(NT // PT):
            act.wait_ge(self.x_var, it + 1)
            nc.scalar.activation(self.dev[:], self.mv[:, :, 1], ACT.Sqrt, bias=sh.eps[:]).then_inc(self.x_dev, 1)
        for j in range(SG // 2):
            keep(Strip(0, 0, 0), j)
        for layer in range(LAYERS):
            for_strips(act, layer, body)
        body(Strip(LAYERS, 0, 0), dense=False)

    def gpsimd(self, pool):
        for it in range(NT // PT):
            xn = self.x_norm[it % 2]
            pool.wait_ge(self.x_scaled, it + 1)
            self.nc.gpsimd.tensor_tensor(xn, xn, self.sh.vec[:, 5:6, :].to_broadcast([P, PT, D]),
                                         ALU.add).then_inc(self.x_shifted, 1)

    def vector(self, dve):
        nc, sh, vec = self.nc, self.sh, self.sh.vec
        steps = [0]

        def link(ins):
            steps[0] += 1
            ins.then_inc(self.prep, 1)
            dve.wait_ge(self.prep, steps[0])

        def hot(strip, g):
            n = strip.s * SG + g
            wait(dve, self.counted, n - HOTS + 1)
            nc.vector.tensor_scalar(self.hot_key[:, g % HOTS, :], sh.iota[:, 0:KW], sh.key_t[:, bass.ds(n, 1)], None,
                                    ALU.is_equal).then_inc(self.hot_done, 1)
            nc.vector.tensor_scalar(self.hot_lo[:, g % HOTS, :], sh.iota[:, 0:P], sh.lo_t[:, bass.ds(n, 1)], None,
                                    ALU.is_equal).then_inc(self.hot_done, 1)

        def finish_y(done, u):
            layer, n, i = done.layer, done.tiles + u, (SW // P) * done.s + u
            y = self.y[:, u, :]
            dve.wait_ge(self.proj_done, n + 1)
            nc.vector.scalar_tensor_tensor(out=y, in0=self.ps_proj[:, 0, :], scalar=self.c_sum[:, layer, bass.ds(i, 1)],
                                           in1=vec[:, layer, :], op0=ALU.mult, op1=ALU.add).then_inc(self.y_part, 1)
            dve.wait_ge(self.y_part, n + 1)
            nc.vector.scalar_tensor_tensor(out=y, in0=self.ps_proj[:, 1, :], scalar=self.c_root[:, layer:layer + 1],
                                           in1=y, op0=ALU.mult, op1=ALU.add).then_inc(self.y_done, 1)
            if layer in NORM_LAYERS:
                m = NORM_LAYERS[layer] * NT + i
                dve.wait_ge(self.res_in[u], 16 * (NORM_LAYERS[layer] * (NT + 1 - u) // 2
                                                  + done.s + 1))
                dve.wait_ge(self.y_done, n + 1)
                nc.vector.tensor_tensor(y, y, self.res[:, u, :], ALU.add).then_inc(self.res_done, 1)
                dve.wait_ge(self.res_done, m + 1)
                nc.vector.bn_stats(self.stats[:, 0, :], y).then_inc(self.stat_done, 1)
                dve.wait_ge(self.stat_done, m + 1)
                nc.vector.memset(self.carry[:], 0.0)
                nc.vector.bn_aggr(self.mv[:, 0, :], self.stats[:, 0, :]).then_inc(self.var_done, 1)

        def finish_z(done, u):
            layer, n, i = done.layer, done.tiles + u, (SW // P) * done.s + u
            y, z = self.y[:, u, :], self.z[:, u, :]
            if layer < LAYERS - 1:
                hi, lo = (self.hp[:, (layer + 1) % 2, bass.ds(i, 1), part, :].rearrange("p a d -> p (a d)")
                          for part in range(2))
            if layer in NORM_LAYERS:
                m = NORM_LAYERS[layer] * NT + i
                dve.wait_ge(self.dev_done, m + 1)
                nc.vector.reciprocal(self.rstd[:, 0:1], self.dev[:, 0:1]).then_inc(self.rstd_done, 1)
                wait(dve, self.z_out[u], 16 * (NORM_LAYERS[layer] * (NT + 1 - u) // 2 + done.s))
                dve.wait_ge(self.rstd_done, m + 1)
                nc.vector.tensor_scalar(z, y, self.mv[:, 0, 0:1], self.rstd[:, 0:1], ALU.subtract,
                                        ALU.mult).then_inc(self.z_done, 1)
                if layer == 0:
                    dve.wait_ge(self.z_done, m + 1)
                    nc.vector.tensor_scalar(hi, z, self.scale[:, 1:2], None, ALU.mult).then_inc(self.hi_done, 1)
                    dve.wait_ge(self.hi_done, n + 1)
                    nc.vector.scalar_tensor_tensor(out=lo, in0=z, scalar=self.scale[:, 1:2], in1=hi, op0=ALU.mult,
                                                   op1=ALU.subtract).then_inc(self.piece_done, 1)
            else:
                dve.wait_ge(self.y_done, n + 1)
                nc.vector.tensor_scalar_max(hi, y, 0.0).then_inc(self.hi_done, 1)
                dve.wait_ge(self.hi_done, n + 1)
                nc.vector.scalar_tensor_tensor(out=lo, in0=y, scalar=0.0, in1=hi, op0=ALU.max,
                                               op1=ALU.subtract).then_inc(self.piece_done, 1)

        def body(strip, dense=True):
            done = strip.before()
            for h in range(NT):
                if dense and strip.layer == 0 and not strip.is_strip(NS - 1):
                    for g in groups_at(h):
                        hot(strip.next(), g)
                for u in range(done.count if done else 0):
                    if h == Y_AT + APART * u:
                        finish_y(done, u)
                    if h == Z_AT + APART * u:
                        finish_z(done, u)

        top = float(D) ** 0.5
        nc.vector.tensor_scalar(self.w_abs.bitcast(I32), sh.w[:, 1:3].rearrange("p l s k d -> p (l s k d)").bitcast(I32),
                                0x7FFFFFFF, None, ALU.bitwise_and).then_inc(self.abs_done, 1)
        link(nc.vector.tensor_scalar(self.vec_abs.bitcast(I32), vec[:].rearrange("p v d -> p (v d)").bitcast(I32),
                                     0x7FFFFFFF, None, ALU.bitwise_and))
        link(nc.vector.tensor_reduce(self.vec_max[:], self.vec_abs.rearrange("p (v d) -> p v d", v=6), AX_X, ALU.max))
        dve.wait_ge(self.rows_done, 1)
        link(nc.vector.tensor_reduce(self.row_max[:], self.ps_proj[:], AX_X, ALU.max))
        link(nc.vector.scalar_tensor_tensor(out=self.bound[:, 0:1], in0=self.vec_max[:, 4:5], scalar=top,
                                            in1=self.vec_max[:, 5:6], op0=ALU.mult, op1=ALU.add))
        link(nc.vector.memset(self.bound[:, 1:2], top))
        link(nc.vector.scalar_tensor_tensor(out=self.bound[:, 2:3], in0=self.row_max[:, 0:1], scalar=top,
                                            in1=self.vec_max[:, 1:2], op0=ALU.mult, op1=ALU.add))
        link(nc.vector.scalar_tensor_tensor(out=self.bound[:, 3:4], in0=self.row_max[:, 1:2],
                                            scalar=self.bound[:, 2:3], in1=self.vec_max[:, 2:3], op0=ALU.mult,
                                            op1=ALU.add))
        link(nc.vector.tensor_scalar_max(self.bound[:], self.bound[:], 1e-20))
        link(nc.vector.tensor_scalar(self.bound[:].bitcast(I32), self.bound[:].bitcast(I32), 0x7F800000, None,
                                     ALU.bitwise_and))
        link(nc.vector.tensor_scalar_mul(self.unscale[:], self.bound[:], 2.0 ** -14))
        link(nc.vector.reciprocal(self.scale[:], self.unscale[:]))
        link(nc.vector.memset(self.after[:], 1.0))
        link(nc.vector.tensor_copy(self.after[:, 1:3], self.scale[:, 2:4]))
        link(nc.vector.tensor_tensor(self.c_root[:], self.unscale[:], self.after[:], ALU.mult))
        for row, factor in ((1, self.after[:, 1:2]), (2, self.after[:, 2:3]), (4, self.scale[:, 0:1]),
                            (5, self.scale[:, 0:1])):
            link(nc.vector.tensor_scalar(vec[:, row, :], vec[:, row, :], factor, None, ALU.mult))

        def pieces(it):
            xn = self.x_norm[it % 2]
            hi, lo = (self.hp[:, 0, it * PT:(it + 1) * PT, part, :] for part in range(2))
            dve.wait_ge(self.x_shifted, it + 1)
            link(nc.vector.tensor_scalar_max(hi, xn, 0.0))
            nc.vector.scalar_tensor_tensor(out=lo, in0=xn, scalar=0.0, in1=hi, op0=ALU.max,
                                           op1=ALU.subtract).then_inc(self.x_pieces, 1)

        for it in range(NT // PT):
            xt, xn = self.x_tiles[it % 2], self.x_norm[it % 2]
            dve.wait_ge(self.x_in[it % 2], 16 * (it // 2 + 1))
            for t in range(PT):
                last = nc.vector.bn_stats(self.stats[:, t, :], xt[:, t, :])
            link(last)
            for t in range(PT):
                last = nc.vector.bn_aggr(self.mv[:, t, :], self.stats[:, t, :])
            last.then_inc(self.x_var, 1)
            if it:
                pieces(it - 1)
            dve.wait_ge(self.x_dev, it + 1)
            link(nc.vector.reciprocal(self.rstd[:], self.dev[:]))
            for t in range(PT):
                last = nc.vector.tensor_scalar(xn[:, t, :], xt[:, t, :], self.mv[:, t, 0:1], self.rstd[:, t:t + 1],
                                               ALU.subtract, ALU.mult)
            last.then_inc(self.x_read, 1)
            dve.wait_ge(self.x_read, it + 1)
            nc.vector.tensor_tensor(xn, xn, vec[:, 4:5, :].to_broadcast([P, PT, D]), ALU.mult).then_inc(self.x_scaled, 1)
        pieces(NT // PT - 1)
        dve.wait_ge(self.deg_in, 16)
        link(nc.vector.tensor_scalar_max(self.rdeg[:], self.deg_n[:], 1.0))
        link(nc.vector.reciprocal(self.deg_n[:], self.rdeg[:]))
        for layer in range(LAYERS):
            link(nc.vector.tensor_scalar(self.c_sum[:, layer, :], self.deg_n[:], self.c_root[:, layer:layer + 1], None,
                                         ALU.mult))
        for g in range(SG):
            hot(Strip(0, 0, 0), g)
        for layer in range(LAYERS):
            for_strips(dve, layer, body)
        body(Strip(LAYERS, 0, 0), dense=False)

    def sync(self, sp):
        nc = self.nc
        strip_bytes = "p h d -> p (h d)"

        def store_a(strip):
            sp.wait_ge(self.a_built, (SG // 2) * (strip.s + 1))
            sp.dma_start(self.a_dram[bass.ds(strip.s, 1)].rearrange("a p n -> p (a n)"),
                         self.a_sb[:, strip.slot].rearrange(strip_bytes)).then_inc(self.a_out[strip.slot], 16)

        def load_a(strip):
            wait(sp, self.agg_done, strip.q - 1)
            sp.dma_start(self.a_sb[:, strip.slot].rearrange(strip_bytes),
                         self.a_dram[bass.ds(strip.s, 1)].rearrange("a p n -> p (a n)")
                         ).then_inc(self.a_in[strip.slot], 16)

        def rows(dram, i):
            return dram[bass.ds(i * P, P), :]

        def body(strip, dense=True):
            done = strip.before()
            layer = strip.layer
            if dense and layer and not strip.is_strip(NS - 1):
                load_a(strip.next())
            if dense and strip.is_strip(NS - 1) and layer < LAYERS - 1:
                if layer == 0:
                    for b in range(2):
                        sp.wait_ge(self.a_out[b], 16 * ((NS + 1 - b) // 2))
                load_a(Strip(layer + 1, 0, 0))
            if done and done.layer in NORM_LAYERS:
                norm = NORM_LAYERS[done.layer]
                first = (SW // P) * done.s
                source = (self.x, self.x1_dram)[norm]
                wait(sp, self.res_done, norm * NT + first)
                for u in range(done.count):
                    sp.dma_start(self.res[:, u, :], rows(source, first + u)).then_inc(self.res_in[u], 16)
            if dense and layer == 0 and not strip.is_strip(NS - 1):
                store_next = strip.next()
            else:
                store_next = None
            if done and done.layer in NORM_LAYERS:
                target = (self.x1_dram, self.out)[norm]
                for u in range(done.count):
                    sp.wait_ge(self.z_done, norm * NT + first + u + 1)
                    sp.dma_start(rows(target, first + u), self.z[:, u, :]).then_inc(self.z_out[u], 16)
            if store_next:
                store_a(store_next)

        sp.dma_start(self.deg_dram.rearrange("(c p j) -> p c j", c=GC, p=GP),
                     self.sh.deg[:]).then_inc(self.deg_out, 16)
        for it in range(NT // PT):
            wait(sp, self.x_read, it - 1)
            sp.dma_start(self.x_tiles[it % 2], self.x[it * PT * P:(it + 1) * PT * P, :].rearrange(
                "(t p) d -> p t d", p=P)).then_inc(self.x_in[it % 2], 16)
            if it == 1:
                sp.wait_ge(self.deg_out, 16)
                with nc.allow_non_contiguous_dma(reason="one degree per partition and node tile"):
                    sp.dma_start(self.deg_n[:], self.deg_dram.rearrange("(t p) -> p t", p=P)).then_inc(self.deg_in, 16)
        store_a(Strip(0, 0, 0))
        for layer in range(LAYERS):
            if layer == LAYERS - 1:
                for u in range(2):
                    sp.wait_ge(self.z_out[u], 16 * ((NT + 1 - u) // 2))
            for_strips(sp, layer, body)
        body(Strip(LAYERS, 0, 0), dense=False)
        for u in range(2):
            sp.wait_ge(self.z_out[u], 2 * 16 * ((NT + 1 - u) // 2))


def build(nc, x, heads, edges, dst_rows, weights, vectors, out):
    with ExitStack() as ctx:
        mem = Mem(nc, ctx)
        sh = Shared(mem)
        with ExitStack() as part:
            find_windows(nc, Mem(nc, part), sh, heads, edges, dst_rows, weights, vectors)
        with ExitStack() as part:
            other = general(nc, Mem(nc, part), sh, x, edges, out)
        fast = Fast(nc, mem, sh, x, out)

        block = ctx.enter_context(nc.Block())

        @block.tensor
        def _(pe):
            dense = pe.value_load(sh.dense[:], min_val=0, max_val=1)
            with pe.If(dense):
                fast.tensor(pe)
            with pe.Else():
                other["tensor"](pe)

        @block.scalar
        def _(act):
            dense = act.value_load(sh.dense[:], min_val=0, max_val=1)
            with act.If(dense):
                fast.scalar(act)
            with act.Else():
                other["scalar"](act)

        @block.vector
        def _(dve):
            dense = dve.value_load(sh.dense[:], min_val=0, max_val=1)
            with dve.If(dense):
                fast.vector(dve)
            with dve.Else():
                other["vector"](dve)

        @block.gpsimd
        def _(pool):
            dense = pool.value_load(sh.dense[:], min_val=0, max_val=1)
            with pool.If(dense):
                fast.gpsimd(pool)
            with pool.Else():
                other["gpsimd"](pool)

        @block.sync
        def _(sp):
            dense = sp.value_load(sh.dense[:], min_val=0, max_val=1)
            with sp.If(dense):
                fast.sync(sp)
            with sp.Else():
                other["sync"](sp)


def kernel(**inputs):
    import numpy as np
    import concourse.bacc as bacc
    from concourse import mybir as mb
    from concourse.bass_utils import run_bass_kernel_spmd as run

    def pad_rows(a, rows, fill):
        a = np.asarray(a)
        return np.concatenate([a, np.full((rows - a.shape[0],) + a.shape[1:], fill, a.dtype)])

    sides = [("L0_gnn_W_l", "L0_gnn_W_r")] + [(f"L1_gnn_W{i}l", f"L1_gnn_W{i}r") for i in (1, 2, 3)]
    w = np.stack([np.stack([np.asarray(inputs[n]).T.reshape(KH, P, D) for n in s]) for s in sides])
    w = np.ascontiguousarray(w.transpose(3, 0, 1, 2, 4))
    vec = np.stack([np.asarray(inputs[n]) for n in
                    ("L0_gnn_b_l", "L1_gnn_b1l", "L1_gnn_b2l", "L1_gnn_b3l", "L0_gnn_gamma", "L0_gnn_beta")])
    src, dst = pad_rows(inputs["src"], EPAD, 0), pad_rows(inputs["dst"], EPAD, NPAD - 1)
    arrays = {
        "x": pad_rows(inputs["x"], NPAD, 0),
        "heads": np.ascontiguousarray(np.broadcast_to(dst[::P], (GP, ET))),
        "edges": np.stack([src, dst], axis=1),
        "dst_rows": dst.reshape(ET, P),
        "weights": w,
        "vectors": np.ascontiguousarray(np.broadcast_to(vec, (P,) + vec.shape)),
    }
    nc = bacc.Bacc("TRN2", target_bir_lowering=False, num_devices=1)
    args = [nc.dram_tensor(f"in_{n}_dram", a.shape, mb.dt.from_np(a.dtype), kind="ExternalInput").ap()
            for n, a in arrays.items()]
    out = nc.dram_tensor("out_0_dram", (NPAD, D), F32, kind="ExternalOutput").ap()
    build(nc, *args, out)
    r = run(nc, [{f"in_{n}_dram": a for n, a in arrays.items()}], core_ids=[0])
    return r.results[0]["out_0_dram"][:NODES]
```

```python
from contextlib import ExitStack

import concourse.bass as bass
from concourse import mybir

P = 128
NODES = 6250
D = 256
EDGES = 106250
NT = -(-NODES // P)
NPAD = NT * P
ET = -(-EDGES // P)
EPAD = ET * P
KH = D // P
LAYERS = 4
EPS = 1e-5
DUMP = NPAD + 1
SW = 256
DT = 2 * NT // 3 + 1
NS = -(-DT * P // SW)
GD = 4
NG = NPAD // GD
SG = SW // GD
GP = 112
GC = NG // GP
GW = 10
CH = 19
SETS = ((0, 5), (5, 10), (10, 15), (15, CH))
CC = -(-(NT - DT) * CH // GP)
CHUNK_WIDTH = [P] + [P // 2] * (CH - 1)
CHUNK_BASE = [0] + [min(max(j * P * NODES // EDGES - P // 4, 0), P // 2) for j in range(1, CH)]
KW = GD * NT
PT = 7
WL = 2 * KH * D
W_BATCH = 4
HOTS = 4
assert GP * GC == NG and NT % PT == 0 and 2 * KW <= 512 and GW * GP >= NS * SG
assert NS * 2 - 1 == DT and NT - DT == NS - 1 and NS % 2 == 1

ALU = mybir.AluOpType
ACT = mybir.ActivationFunctionType
AX_X = mybir.AxisListType.X
F16 = mybir.dt.float16
F32 = mybir.dt.float32
I32 = mybir.dt.int32
U32 = mybir.dt.uint32


class Mem:

    def __init__(self, nc, ctx):
        self.nc, self.ctx = nc, ctx

    def sb(self, name, shape, dt=F32):
        return self.ctx.enter_context(self.nc.sbuf_tensor(name, shape, dt))

    def ps(self, name, shape, dt=F32):
        return self.ctx.enter_context(self.nc.psum_tensor(name, shape, dt))

    def sem(self, name):
        return self.ctx.enter_context(self.nc.semaphore(name))


class Shared:

    def __init__(self, mem):
        self.ident = mem.sb("ident", [P, P])
        self.ident16 = mem.sb("ident16", [P, P], F16)
        self.ones = mem.sb("ones", [P, P])
        self.eps = mem.sb("eps", [P, 1])
        self.iota = mem.sb("iota", [P, KW], F16)
        self.vec = mem.sb("vec", [P, 6, D])
        self.key_t = mem.sb("key_t", [P, GW * GP], F16)
        self.lo_t = mem.sb("lo_t", [P, GW * GP], F16)
        self.chunk_src = mem.sb("chunk_src", [P, CC * GP], I32)
        self.chunk_dst = mem.sb("chunk_dst", [P, CC * GP])
        self.deg = mem.sb("deg", [GP, GC, GD])
        self.dense = mem.sb("dense", [1, 1], I32)


def wait(eng, sem, value):
    if isinstance(value, int) and value <= 0:
        return
    eng.wait_ge(sem, value)


class Features:

    def __init__(self, nc, mem, part, shared, x, weights):
        self.nc, self.sh, self.x, self.weights = nc, shared, x, weights
        sb, sem = mem.sb, mem.sem
        self.h_dram = [nc.dram_tensor(f"h_dram{i}", (NPAD, 2 * D), F16, kind="Internal").ap()
                       for i in range(LAYERS)]
        self.hp = sb("hp", [P, 2, NT, 2, D], F16)
        self.scale = sb("scale", [P, LAYERS])
        self.c_root = sb("c_root", [P, LAYERS])
        self.w_dram = nc.dram_tensor("w_dram", (P, LAYERS, 2 * WL), F16, kind="Internal").ap()
        self.h_out = sem("h_out")
        sb, sem, ps = part.sb, part.sem, part.ps
        self.unscale = sb("p_unscale", [P, LAYERS])
        self.after = sb("p_after", [P, LAYERS])
        self.bound = sb("p_bound", [P, LAYERS])
        self.vec_abs = sb("p_vec_abs", [P, 6 * D])
        self.vec_max = sb("p_vec_max", [P, 6])
        self.stats = sb("p_stats", [P, PT, 6])
        self.mv = sb("p_mv", [P, PT, 2])
        self.dev = sb("p_dev", [P, PT])
        self.rstd = sb("p_rstd", [P, PT])
        self.shift = sb("p_shift", [P, PT])
        work = self.hp[:, 1].rearrange("p t c d -> p (t c d)").bitcast(F32)
        n = PT * D
        self.x_tiles = [work[:, b * n:(b + 1) * n].rearrange("p (t d) -> p t d", t=PT) for b in range(2)]
        self.x_norm = [work[:, (2 + b) * n:(3 + b) * n].rearrange("p (t d) -> p t d", t=PT) for b in range(2)]
        self.w_all = work[:, 4 * n:4 * n + LAYERS * WL].rearrange("p (l n) -> p l n", l=LAYERS)
        first, tiles = W_BATCH * PT, LAYERS * WL // D
        room = self.hp[:, 0, first:first + tiles].rearrange("p t c d -> p (t c d)")
        self.w_abs = room.bitcast(F32)
        self.w_parts = room.rearrange("p (l c n) -> p l c n", l=LAYERS, c=2)
        self.w_max = sb("p_w_max", [P, LAYERS])
        self.w_unscale = sb("p_w_unscale", [P, LAYERS])
        self.w_scale = sb("p_w_scale", [P, LAYERS])
        self.x_in = [sem(f"p_x_in{b}") for b in range(2)]
        self.bound_in = sem("p_bound_in")
        self.steps_done = sem("p_steps_done")
        self.abs_done = sem("p_abs_done")
        self.w_split = sem("p_w_split")
        self.w_out = sem("w_out")
        self.rows_done = sem("p_rows_done")
        self.x_var = sem("p_x_var")
        self.x_dev = sem("p_x_dev")
        self.x_shift = sem("p_x_shift")
        self.x_normed = sem("p_x_normed")
        self.x_pieces = sem("p_x_pieces")
        self.steps = 0

    def link(self, dve, ins):
        self.steps += 1
        ins.then_inc(self.steps_done, 1)
        dve.wait_ge(self.steps_done, self.steps)

    def load_weights(self, sp):
        sp.dma_start(self.w_all, self.weights.rearrange("p l s k d -> p l (s k d)")).then_inc(self.bound_in, 16)

    def store_weights(self, sp):
        sp.wait_ge(self.w_split, 1)
        sp.dma_start(self.w_dram, self.w_parts.rearrange("p l c n -> p l (c n)")).then_inc(self.w_out, 16)

    def load(self, sp, it):
        wait(sp, self.x_normed, it - 1)
        sp.dma_start(self.x_tiles[it % 2], self.x[it * PT * P:(it + 1) * PT * P, :].rearrange(
            "(t p) d -> p t d", p=P)).then_inc(self.x_in[it % 2], 16)

    def store(self, sp, it):
        sp.wait_ge(self.x_pieces, it + 1)
        sp.dma_start(self.h_dram[0][it * PT * P:(it + 1) * PT * P, :].rearrange("(t p) d -> p t d", p=P),
                     self.hp[:, 0, it * PT:(it + 1) * PT].rearrange("p t c d -> p t (c d)")
                     ).then_inc(self.h_out, 16)

    def sum_rows(self, pe, banks):
        pe.wait_ge(self.abs_done, 1)
        per = WL // D
        for j in range(LAYERS * per):
            layer = j // per
            last = self.nc.tensor.matmul(banks[layer // 2][:, layer % 2 * D:(layer % 2 + 1) * D], self.sh.ones[:],
                                         self.w_abs[:, j * D:(j + 1) * D], start=(j % per == 0),
                                         stop=(j % per == per - 1))
        last.then_inc(self.rows_done, 1)

    def magnitudes(self, dve):
        nc, vec = self.nc, self.sh.vec
        dve.wait_ge(self.bound_in, 16)
        nc.vector.tensor_scalar(self.w_abs.bitcast(I32), self.w_all.rearrange("p l n -> p (l n)").bitcast(I32),
                                0x7FFFFFFF, None, ALU.bitwise_and).then_inc(self.abs_done, 1)
        self.link(dve, nc.vector.tensor_scalar(
            self.vec_abs[:].bitcast(I32), vec[:].rearrange("p v d -> p (v d)").bitcast(I32), 0x7FFFFFFF, None,
            ALU.bitwise_and))
        self.link(dve, nc.vector.tensor_reduce(self.vec_max[:], self.vec_abs[:].rearrange("p (v d) -> p v d", v=6),
                                               AX_X, ALU.max))

    def scales(self, dve, banks):
        nc, vec, top = self.nc, self.sh.vec, float(D) ** 0.5

        def link(ins):
            self.link(dve, ins)

        dve.wait_ge(self.rows_done, 1)
        for b in range(2):
            link(nc.vector.tensor_reduce(self.w_max[:, 2 * b:2 * b + 2], banks[b][:].rearrange("p (l d) -> p l d", l=2),
                                         AX_X, ALU.max))
        link(nc.vector.scalar_tensor_tensor(out=self.bound[:, 0:1], in0=self.vec_max[:, 4:5], scalar=top,
                                            in1=self.vec_max[:, 5:6], op0=ALU.mult, op1=ALU.add))
        link(nc.vector.memset(self.bound[:, 1:2], top))
        link(nc.vector.scalar_tensor_tensor(out=self.bound[:, 2:3], in0=self.w_max[:, 1:2], scalar=top,
                                            in1=self.vec_max[:, 1:2], op0=ALU.mult, op1=ALU.add))
        link(nc.vector.scalar_tensor_tensor(out=self.bound[:, 3:4], in0=self.w_max[:, 2:3],
                                            scalar=self.bound[:, 2:3], in1=self.vec_max[:, 2:3], op0=ALU.mult,
                                            op1=ALU.add))
        link(nc.vector.tensor_scalar_max(self.bound[:], self.bound[:], 1e-20))
        link(nc.vector.tensor_scalar(self.bound[:].bitcast(I32), self.bound[:].bitcast(I32), 0x7F800000, None,
                                     ALU.bitwise_and))
        link(nc.vector.tensor_scalar_mul(self.unscale[:], self.bound[:], 2.0 ** -14))
        link(nc.vector.reciprocal(self.scale[:], self.unscale[:]))
        link(nc.vector.memset(self.after[:], 1.0))
        link(nc.vector.tensor_copy(self.after[:, 1:3], self.scale[:, 2:4]))
        link(nc.vector.tensor_tensor(self.c_root[:], self.unscale[:], self.after[:], ALU.mult))
        link(nc.vector.tensor_scalar_max(self.w_max[:], self.w_max[:], 1e-20))
        link(nc.vector.tensor_scalar(self.w_max[:].bitcast(I32), self.w_max[:].bitcast(I32), 0x7F800000, None,
                                     ALU.bitwise_and))
        link(nc.vector.tensor_scalar_mul(self.w_unscale[:], self.w_max[:], 2.0 ** -14))
        link(nc.vector.reciprocal(self.w_scale[:], self.w_unscale[:]))
        link(nc.vector.tensor_tensor(self.c_root[:], self.c_root[:], self.w_unscale[:], ALU.mult))
        for row, factor in ((1, self.after[:, 1:2]), (2, self.after[:, 2:3]), (4, self.scale[:, 0:1]),
                            (5, self.scale[:, 0:1])):
            link(nc.vector.tensor_scalar(vec[:, row, :], vec[:, row, :], factor, None, ALU.mult))

    def split_weights(self, dve):
        nc = self.nc

        def link(ins):
            self.link(dve, ins)

        for layer in range(LAYERS):
            hi, lo = (self.w_parts[:, layer, part, :] for part in range(2))
            link(nc.vector.tensor_scalar(hi, self.w_all[:, layer, :], self.w_scale[:, layer:layer + 1], None,
                                         ALU.mult))
            ins = nc.vector.scalar_tensor_tensor(out=lo, in0=self.w_all[:, layer, :],
                                                 scalar=self.w_scale[:, layer:layer + 1], in1=hi, op0=ALU.mult,
                                                 op1=ALU.subtract)
            if layer < LAYERS - 1:
                link(ins)
        ins.then_inc(self.w_split, 1)

    def moments(self, dve, it):
        xt = self.x_tiles[it % 2]
        dve.wait_ge(self.x_in[it % 2], 16 * (it // 2 + 1))
        for t in range(PT):
            last = self.nc.vector.bn_stats(self.stats[:, t, :], xt[:, t, :])
        self.link(dve, last)
        wait(dve, self.x_normed, it)
        for t in range(PT):
            last = self.nc.vector.bn_aggr(self.mv[:, t, :], self.stats[:, t, :])
        last.then_inc(self.x_var, 1)

    def deviations(self, act, it):
        act.wait_ge(self.x_var, it + 1)
        self.nc.scalar.activation(self.dev[:], self.mv[:, :, 1], ACT.Sqrt, bias=self.sh.eps[:]).then_inc(self.x_dev, 1)

    def factors(self, dve, it):
        dve.wait_ge(self.x_dev, it + 1)
        self.link(dve, self.nc.vector.reciprocal(self.rstd[:], self.dev[:]))
        self.nc.vector.scalar_tensor_tensor(out=self.shift[:], in0=self.mv[:, :, 0], scalar=-1.0, in1=self.rstd[:],
                                            op0=ALU.mult, op1=ALU.mult).then_inc(self.x_shift, 1)

    def norm(self, act, it):
        act.wait_ge(self.x_shift, it + 1)
        wait(act, self.x_pieces, it - 1)
        for t in range(PT):
            last = self.nc.scalar.activation(self.x_norm[it % 2][:, t, :], self.x_tiles[it % 2][:, t, :],
                                             ACT.Identity, bias=self.shift[:, t:t + 1], scale=self.rstd[:, t:t + 1])
        last.then_inc(self.x_normed, 1)

    def pieces(self, dve, it):
        nc, vec, xn = self.nc, self.sh.vec, self.x_norm[it % 2]
        hi, lo = (self.hp[:, 0, it * PT:(it + 1) * PT, part, :] for part in range(2))
        if it == W_BATCH:
            dve.wait_ge(self.w_out, 16)
        dve.wait_ge(self.x_normed, it + 1)
        self.link(dve, nc.vector.tensor_tensor(xn, xn, vec[:, 4:5, :].to_broadcast([P, PT, D]), ALU.mult))
        self.link(dve, nc.vector.tensor_tensor(xn, xn, vec[:, 5:6, :].to_broadcast([P, PT, D]), ALU.add))
        self.link(dve, nc.vector.tensor_scalar_max(hi, xn, 0.0))
        nc.vector.scalar_tensor_tensor(out=lo, in0=xn, scalar=0.0, in1=hi, op0=ALU.max,
                                       op1=ALU.subtract).then_inc(self.x_pieces, 1)


def find_windows(nc, mem, sh, feat, heads, edges, dst_rows, plan, vectors):
    heads_i = mem.sb("w_heads_i", [GP, ET], I32)
    heads_f = mem.sb("w_heads_f", [GP, ET])
    below = mem.sb("w_below", [GP, 2, ET])
    plan_t = mem.sb("w_plan", [GP, 4, CC])
    first_dst = mem.sb("w_first_dst", [GP, GC])
    row_f = mem.sb("w_row_f", [GP, GC + CC])
    row_i = mem.sb("w_row_i", [GP, GC + CC], I32)
    chunk = mem.sb("w_chunk", [GP, CC, 2 * P], I32)
    chunk_src = mem.sb("w_chunk_src", [GP, CC, P])
    chunk_dst = mem.sb("w_chunk_dst", [GP, CC, P])
    inside = mem.sb("w_inside", [GP, CC, P])
    strips_deg = mem.sb("w_strips_deg", [GP, 2])
    row_dst = mem.sb("w_row_dst", [GP, GC, P], I32)
    in_row = mem.sb("w_in_row", [GP, GC])
    start_f = mem.sb("w_start_f", [GP, GC])
    start_i = mem.sb("w_start_i", [GP, GC], I32)
    window = mem.sb("w_window", [GP, GC, 2 * P], I32)
    rel = mem.sb("w_rel", [GP, GC, P])
    bits = mem.sb("w_bits", [GP, GC, P], I32)
    low_bits = mem.sb("w_low_bits", [GP, GC, P], I32)
    lo = mem.sb("w_lo", [GP, GC, P])
    key = mem.sb("w_key", [GP, GC, P])
    total = mem.sb("w_total", [GP, 2])
    both = mem.sb("w_both", [1, 2])
    ps_t = [mem.ps(f"w_ps{i}", [P, 512]) for i in range(8)]

    made = mem.sem("w_made")
    heads_in = mem.sem("w_heads_in")
    params_in = mem.sem("w_params_in")
    v = mem.sem("w_v")
    compared = mem.sem("w_compared")
    ranked = mem.sem("w_ranked")
    rows_ready = mem.sem("w_rows_ready")
    rows_in = mem.sem("w_rows_in")
    starts_ready = mem.sem("w_starts_ready")
    windows_in = mem.sem("w_windows_in")
    lo_ready = mem.sem("w_lo_ready")
    key_ready = mem.sem("w_key_ready")
    chunks_in = mem.sem("w_chunks_in")
    chunks_ready = mem.sem("w_chunks_ready")
    turned = mem.sem("w_turned")
    total_ready = mem.sem("w_total_ready")
    total_done = mem.sem("w_total_done")
    copied = mem.sem("w_copied")
    PER = 4
    BATCHES = NT // PT
    FIRST, SECOND = 2, 2
    TURNS = ((chunks_ready, chunk_src, CC, sh.chunk_src), (chunks_ready, chunk_dst, CC, sh.chunk_dst),
             (lo_ready, lo, GW, sh.lo_t), (key_ready, key, GW, sh.key_t))
    BANKS = [(ready, source, i, min(PER, n - i), target) for ready, source, n, target in TURNS
             for i in range(0, n, PER)]
    assert len(BANKS) <= 8

    def wide(columns, n=GC):
        return columns.unsqueeze(2).to_broadcast([GP, n, P])

    with nc.Block() as block:
        @block.sync
        def _(sp):
            sp.dma_start(heads_i[:], heads).then_inc(heads_in, 16)
            sp.dma_start(plan_t[:].rearrange("p a c -> p (a c)"), plan.rearrange("p a c -> p (a c)")
                         ).then_inc(heads_in, 16)
            feat.load_weights(sp)
            sp.dma_start(sh.vec[:].rearrange("p v d -> p (v d)"),
                         vectors.rearrange("p v d -> p (v d)")).then_inc(params_in, 16)
            for it in range(BATCHES):
                feat.load(sp, it)
                if it == W_BATCH - 1:
                    feat.store_weights(sp)
                if it >= 2:
                    feat.store(sp, it - 2)
            feat.store(sp, BATCHES - 2)
            feat.store(sp, BATCHES - 1)
            sp.wait_ge(feat.w_out, 16)

        @block.gpsimd
        def _(pool):
            nc.gpsimd.iota(first_dst[:], pattern=[[GD * GP, GC]], base=0, channel_multiplier=GD,
                           allow_small_or_imprecise_dtypes=True).then_inc(made, 1)
            nc.gpsimd.memset(sh.ident[:], 0.0).then_inc(made, 1)
            nc.gpsimd.iota(sh.iota[:], pattern=[[1, KW]], base=0, channel_multiplier=0,
                           allow_small_or_imprecise_dtypes=True).then_inc(made, 1)
            nc.gpsimd.memset(sh.ones[:], 1.0).then_inc(made, 1)
            nc.gpsimd.memset(sh.eps[:], EPS).then_inc(made, 1)
            pool.wait_ge(made, 5)
            nc.gpsimd.affine_select(out=sh.ident[:], in_=sh.ident[:], compare_op=ALU.not_equal, fill=1.0, base=0,
                                    pattern=[[-1, P]], channel_multiplier=1).then_inc(made, 1)
            pool.wait_ge(made, 6)
            nc.gpsimd.tensor_copy(sh.ident16[:], sh.ident[:]).then_inc(made, 1)
            pool.wait_ge(rows_ready, 1)
            for c in range(GC):
                pool.indirect_dma_start(
                    out=row_dst[:, c, :], out_offset=None, in_=dst_rows,
                    in_offset=bass.IndirectOffsetOnAxis(ap=row_i[:, c:c + 1].bitcast(U32), axis=0)
                ).then_inc(rows_in, 16)
            for c in range(CC):
                pool.indirect_dma_start(
                    out=chunk[:, c, :], out_offset=None, in_=edges.rearrange("(n e) t -> n (e t)", e=P),
                    in_offset=bass.IndirectOffsetOnAxis(ap=row_i[:, GC + c:GC + c + 1].bitcast(U32), axis=0)
                ).then_inc(chunks_in, 16)
            pool.wait_ge(starts_ready, 1)
            for c in range(GC):
                pool.indirect_dma_start(
                    out=window[:, c, :], out_offset=None, in_=edges.rearrange("n (t o) -> (n t) o", o=1),
                    in_offset=bass.IndirectOffsetOnAxis(ap=start_i[:, c:c + 1].bitcast(U32), axis=0)
                ).then_inc(windows_in, 16)

        @block.scalar
        def _(act):
            for c in range(GC + CC):
                act.wait_ge(compared, c + 1)
                nc.scalar.activation(below[:, c % 2, :], below[:, c % 2, :], ACT.Copy,
                                     accum_out=row_f[:, c:c + 1]).then_inc(ranked, 1)
            for it in range(FIRST + SECOND):
                feat.deviations(act, it)
                feat.norm(act, it)
            for b, (_, _, i, n, target) in enumerate(BANKS):
                act.wait_ge(turned, b + 1)
                nc.scalar.activation(target[:, i * GP:(i + n) * GP], ps_t[b][:, 0:n * GP],
                                     ACT.Copy).then_inc(copied, 1)
            for it in range(FIRST + SECOND, BATCHES):
                feat.deviations(act, it)
                feat.norm(act, it)

        @block.tensor
        def _(pe):
            pe.wait_ge(made, 7)
            feat.sum_rows(pe, ps_t[6:8])
            for b, (ready, source, i, n, _) in enumerate(BANKS):
                pe.wait_ge(ready, 1)
                for c in range(n):
                    last = nc.tensor.transpose(ps_t[b][:, c * GP:(c + 1) * GP], source[:, i + c, :],
                                               sh.ident[0:GP, 0:GP])
                last.then_inc(turned, 1)
            pe.wait_ge(total_ready, 1)
            pe.wait_ge(copied, 1)
            nc.tensor.matmul(ps_t[0][0:1, 0:2], sh.ones[0:GP, 0:1], total[:], start=True, stop=True).then_inc(total_done, 1)

        @block.vector
        def _(dve):
            steps = [0]

            def link(ins):
                steps[0] += 1
                ins.then_inc(v, 1)
                dve.wait_ge(v, steps[0])

            def batches(start, end):
                for it in range(start, end + 1):
                    if it < end:
                        feat.moments(dve, it)
                    if it > start:
                        feat.pieces(dve, it - 1)
                    if it < end:
                        feat.factors(dve, it)

            dve.wait_ge(heads_in, 32)
            link(nc.vector.tensor_copy(heads_f[:], heads_i[:]))
            dve.wait_ge(made, 1)
            for c in range(GC + CC):
                first = first_dst[:, c:c + 1] if c < GC else plan_t[:, 0, c - GC:c - GC + 1]
                if c >= 2:
                    dve.wait_ge(ranked, c - 1)
                nc.vector.tensor_scalar(below[:, c % 2, :], heads_f[:], first, None,
                                        ALU.is_lt).then_inc(compared, 1)
            dve.wait_ge(ranked, GC + CC)
            link(nc.vector.tensor_scalar(row_f[:], row_f[:], -1.0, 0.0, ALU.add, ALU.max))
            link(nc.vector.tensor_tensor(row_f[:, GC:GC + CC], row_f[:, GC:GC + CC], plan_t[:, 1, :], ALU.add))
            nc.vector.tensor_copy(row_i[:], row_f[:]).then_inc(rows_ready, 1)
            dve.wait_ge(params_in, 16)
            feat.magnitudes(dve)
            feat.scales(dve, ps_t[6:8])
            batches(0, FIRST)
            dve.wait_ge(rows_in, 16 * GC)
            link(nc.vector.tensor_tensor(rel[:], row_dst[:], wide(first_dst[:]), ALU.is_lt))
            link(nc.vector.tensor_reduce(in_row[:], rel[:], AX_X, ALU.add))
            link(nc.vector.scalar_tensor_tensor(out=start_f[:], in0=row_f[:, 0:GC], scalar=float(P), in1=in_row[:],
                                                op0=ALU.mult, op1=ALU.add))
            link(nc.vector.tensor_scalar(start_f[:], start_f[:], float(EPAD - P), 2.0, ALU.min, ALU.mult))
            nc.vector.tensor_copy(start_i[:], start_f[:]).then_inc(starts_ready, 1)
            feat.split_weights(dve)
            batches(FIRST, FIRST + SECOND)
            dve.wait_ge(chunks_in, 16 * CC)
            pairs = chunk[:].rearrange("p c (e t) -> p c e t", t=2)
            link(nc.vector.tensor_copy(chunk_src[:], pairs[:, :, :, 0]))
            nc.vector.tensor_tensor(chunk_dst[:], pairs[:, :, :, 1], wide(plan_t[:, 2, :], CC),
                                    ALU.subtract).then_inc(chunks_ready, 1)
            dve.wait_ge(chunks_ready, 1)
            link(nc.vector.tensor_tensor(inside[:], chunk_dst[:], wide(plan_t[:, 3, :], CC), ALU.is_lt))
            link(nc.vector.scalar_tensor_tensor(out=inside[:], in0=chunk_dst[:], scalar=0.0, in1=inside[:],
                                                op0=ALU.is_ge, op1=ALU.mult))
            link(nc.vector.tensor_reduce(total[:, 1:2], inside[:].rearrange("p c e -> p (c e)"), AX_X, ALU.add))
            dve.wait_ge(windows_in, 16 * GC)
            pairs = window[:].rearrange("p c (e t) -> p c e t", t=2)
            link(nc.vector.tensor_scalar(low_bits[:], pairs[:, :, :, 0], P - 1, None, ALU.bitwise_and))
            nc.vector.tensor_copy(lo[:], low_bits[:]).then_inc(lo_ready, 1)
            nc.vector.tensor_scalar(bits[:], pairs[:, :, :, 0], 7, None, ALU.logical_shift_right).then_inc(v, 1)
            steps[0] += 1
            link(nc.vector.tensor_tensor(rel[:], pairs[:, :, :, 1], wide(first_dst[:]), ALU.subtract))
            nc.vector.scalar_tensor_tensor(out=key[:], in0=rel[:], scalar=float(NT), in1=bits[:], op0=ALU.mult,
                                           op1=ALU.add).then_inc(key_ready, 1)
            batches(FIRST + SECOND, BATCHES)
            for j in range(GD):
                link(nc.vector.tensor_scalar(row_dst[:].bitcast(F32), rel[:], float(j), None, ALU.is_equal))
                link(nc.vector.tensor_reduce(sh.deg[:, :, j], row_dst[:].bitcast(F32), AX_X, ALU.add))
            whole, rest = DT * P // GD // GP, DT * P // GD % GP
            flat = sh.deg[:].rearrange("p c j -> p (c j)")
            link(nc.vector.tensor_reduce(strips_deg[:, 0:1], flat[:, 0:GD * whole], AX_X, ALU.add))
            link(nc.vector.memset(strips_deg[:, 1:2], 0.0))
            link(nc.vector.tensor_reduce(strips_deg[0:rest, 1:2], flat[0:rest, GD * whole:GD * (whole + 1)], AX_X,
                                         ALU.add))
            link(nc.vector.tensor_tensor(total[:, 1:2], total[:, 1:2], strips_deg[:, 0:1], ALU.add))
            link(nc.vector.tensor_tensor(total[:, 1:2], total[:, 1:2], strips_deg[:, 1:2], ALU.add))
            nc.vector.tensor_reduce(total[:, 0:1], flat, AX_X, ALU.add).then_inc(total_ready, 1)
            dve.wait_ge(total_done, 1)
            link(nc.vector.tensor_scalar(both[:], ps_t[0][0:1, 0:2], float(EPAD), None, ALU.is_equal))
            link(nc.vector.tensor_tensor(sh.dense[:], both[:, 0:1], both[:, 1:2], ALU.mult))


def general(nc, mem, shared, x, edges, weights, vectors, out):
    ident = shared.ident
    vec = mem.sb("g_vec", [P, 6, D])
    w = mem.sb("g_w", [P, LAYERS, 2, KH, D])
    w_in = mem.sem("g_w_in")
    h_dram = [nc.dram_tensor(f"g_h{i}", (NPAD, D), F32, kind="Internal").ap() for i in range(LAYERS)]
    agg_dram = nc.dram_tensor("g_agg", (NPAD, D + 1), F32, kind="Internal").ap()
    earlier = mem.sb("g_earlier", [P, P])
    zero = mem.sb("g_zero", [P, D + 1])
    pair = mem.sb("g_pair", [P, 2], I32)
    put_idx = mem.sb("g_put_idx", [P, 1], I32)
    dst_f = mem.sb("g_dst_f", [P, 1])
    dst_wide = mem.sb("g_dst_wide", [P, P])
    same = mem.sb("g_same", [P, P])
    before = mem.sb("g_before", [P, P])
    repeats = mem.sb("g_repeats", [P, 1])
    put_f = mem.sb("g_put_f", [P, 1])
    msg = mem.sb("g_msg", [P, D + 1])
    old = mem.sb("g_old", [P, D + 1])
    new = mem.sb("g_new", [P, D + 1])
    h_t = mem.sb("g_h_t", [P, D])
    agg_t = mem.sb("g_agg_t", [P, D + 1])
    res_t = mem.sb("g_res_t", [P, D])
    mean_t = mem.sb("g_mean_t", [P, D])
    turned = mem.sb("g_turned", [P, 2, KH, P])
    y = mem.sb("g_y", [P, D])
    z = mem.sb("g_z", [P, D])
    stats = mem.sb("g_stats", [P, 6])
    mv = mem.sb("g_mv", [P, 2])
    col = mem.sb("g_col", [P, 4])
    spare = mem.sb("g_spare", [P, 1])
    spare_pool = mem.sb("g_spare_pool", [P, 2])
    ps_dst = mem.ps("g_ps_dst", [P, P])
    ps_sum = mem.ps("g_ps_sum", [P, D + 1])
    ps_turn = mem.ps("g_ps_turn", [P, 2, KH, P])
    ps_out = mem.ps("g_ps_out", [P, D])

    ready = mem.sem("g_ready")
    made = mem.sem("g_made")
    paced = mem.sem("g_paced")
    cleared = mem.sem("g_cleared")
    idx_in = mem.sem("g_idx_in")
    msg_in = mem.sem("g_msg_in")
    old_in = mem.sem("g_old_in")
    put_out = mem.sem("g_put_out")
    turned_dst = mem.sem("g_turned_dst")
    summed = mem.sem("g_summed")
    v = mem.sem("g_v")
    node_in = mem.sem("g_node_in")
    node_out = mem.sem("g_node_out")
    turn_done = mem.sem("g_turn_done")
    proj_done = mem.sem("g_proj_done")
    root = mem.sem("g_root")

    EDGE_STEPS = 8
    PREP_STEPS = 8
    NODE_STEPS = [11, 4, 4, 11]

    def v_at_edges(layer):
        return 1 + NT * PREP_STEPS + sum(ET * EDGE_STEPS + NT * s for s in NODE_STEPS[:layer])

    def v_at_nodes(layer):
        return v_at_edges(layer) + ET * EDGE_STEPS

    def rows(dram, i):
        return dram[bass.ts(i, P), :]

    def gpsimd(pool):
        nc.gpsimd.memset(earlier[:], 1.0).then_inc(made, 1)
        pool.wait_ge(made, 1)
        nc.gpsimd.affine_select(out=earlier[:], in_=earlier[:], compare_op=ALU.is_gt, fill=0.0, base=0,
                                pattern=[[-1, P]], channel_multiplier=1).then_inc(ready, 1)
        def pace():
            nc.gpsimd.tensor_tensor(spare_pool[:, 0:1], spare_pool[:, 1:2], spare_pool[:, 1:2],
                                    ALU.add).then_inc(paced, 1)

        nc.gpsimd.memset(spare_pool[:], 0.0).then_inc(paced, 1)
        for layer in range(LAYERS):
            first = ET * layer
            pool.wait_ge(cleared, 16 * NT * (layer + 1))
            pool.wait_ge(node_out, 16 * NT * (layer + 1))
            with pool.Fori(0, ET) as t:
                pool.wait_ge(paced, 2 * (t + first) + 1)
                pool.wait_ge(idx_in, 16 * (t + first) + 16)
                pace()
                pool.indirect_dma_start(
                    out=msg[:, 0:D], out_offset=None, in_=h_dram[layer],
                    in_offset=bass.IndirectOffsetOnAxis(ap=pair[:, 0:1].bitcast(U32), axis=0),
                    bounds_check=NPAD - 1, oob_is_err=False).then_inc(msg_in, 16)
                pool.indirect_dma_start(
                    out=old[:], out_offset=None, in_=agg_dram,
                    in_offset=bass.IndirectOffsetOnAxis(ap=pair[:, 1:2].bitcast(U32), axis=0),
                    bounds_check=NPAD - 1, oob_is_err=False).then_inc(old_in, 16)
                pool.wait_ge(paced, 2 * (t + first) + 2)
                pool.wait_ge(v, t * EDGE_STEPS + v_at_edges(layer) + EDGE_STEPS)
                pace()
                pool.indirect_dma_start(
                    out=agg_dram, out_offset=bass.IndirectOffsetOnAxis(ap=put_idx[:].bitcast(U32), axis=0),
                    in_=new[:], in_offset=None,
                    bounds_check=NPAD - 1, oob_is_err=False).then_inc(put_out, 16)

    def sync(sp):
        sp.dma_start(w[:].rearrange("p l s k d -> p (l s k d)"),
                     weights.rearrange("p l s k d -> p (l s k d)")).then_inc(w_in, 16)
        sp.dma_start(vec[:].rearrange("p v d -> p (v d)"), vectors.rearrange("p v d -> p (v d)")).then_inc(w_in, 16)
        sp.dma_start(h_t[:], rows(x, 0)).then_inc(node_in, 16)
        with sp.Fori(0, NT - 1) as i:
            sp.wait_ge(v, i * PREP_STEPS + 1 + PREP_STEPS)
            sp.dma_start(rows(h_dram[0], i), y[:]).then_inc(node_out, 16)
            sp.wait_ge(node_out, 16 * i + 16)
            sp.dma_start(h_t[:], rows(x, i + 1)).then_inc(node_in, 16)
        sp.wait_ge(v, NT * PREP_STEPS + 1)
        sp.dma_start(rows(h_dram[0], NT - 1), y[:]).then_inc(node_out, 16)
        for layer in range(LAYERS):
            res = {0: x, 3: h_dram[1]}.get(layer)
            target = h_dram[layer + 1] if layer < LAYERS - 1 else out
            n_in = 3 if res is not None else 2
            sp.wait_ge(v, 1)
            sp.wait_ge(node_out, 16 * NT * (layer + 1))
            with sp.Fori(0, NT) as i:
                sp.dma_start(rows(agg_dram, i), zero[:]).then_inc(cleared, 16)
            sp.dma_start(pair[:], edges[0:P, :]).then_inc(idx_in, 16)
            with sp.Fori(1, ET) as t:
                sp.wait_ge(put_out, 16 * (t + ET * layer))
                sp.dma_start(pair[:], edges[bass.ts(t, P), :]).then_inc(idx_in, 16)
            sp.wait_ge(put_out, 16 * ET * (layer + 1))
            with sp.Fori(0, NT) as i:
                sp.wait_ge(node_out, 16 * i + 16 * NT * (layer + 1))
                sp.dma_start(agg_t[:], rows(agg_dram, i)).then_inc(node_in, 16)
                sp.dma_start(h_t[:], rows(h_dram[layer], i)).then_inc(node_in, 16)
                if res is not None:
                    sp.dma_start(res_t[:], rows(res, i)).then_inc(node_in, 16)
                sp.wait_ge(v, i * NODE_STEPS[layer] + v_at_nodes(layer) + NODE_STEPS[layer])
                sp.dma_start(rows(target, i), y[:]).then_inc(node_out, 16)
        sp.wait_ge(node_out, 16 * NT * (LAYERS + 1))

    def scalar(act):
        with act.Fori(0, NT) as i:
            act.wait_ge(v, i * PREP_STEPS + 1 + 3)
            nc.scalar.activation(col[:, 1:2], col[:, 0:1], ACT.Sqrt).then_inc(root, 1)
        for layer in (0, 3):
            with act.Fori(0, NT) as i:
                act.wait_ge(v, i * NODE_STEPS[layer] + v_at_nodes(layer) + 8)
                nc.scalar.activation(col[:, 1:2], col[:, 0:1], ACT.Sqrt).then_inc(root, 1)

    def vector(dve):
        def norm(source, at, roots):
            nc.vector.bn_stats(stats[:], source).then_inc(v, 1)
            dve.wait_ge(v, at + 1)
            nc.vector.memset(spare[:], 0.0)
            nc.vector.bn_aggr(mv[:], stats[:]).then_inc(v, 1)
            dve.wait_ge(v, at + 2)
            nc.vector.tensor_scalar_add(col[:, 0:1], mv[:, 1:2], EPS).then_inc(v, 1)
            dve.wait_ge(root, roots)
            nc.vector.reciprocal(col[:, 2:3], col[:, 1:2]).then_inc(v, 1)
            dve.wait_ge(v, at + 4)
            return nc.vector.tensor_scalar(z[:] if source is not y[:] else y[:], source, mv[:, 0:1],
                                           col[:, 2:3], ALU.subtract, ALU.mult)

        nc.vector.memset(msg[:, D:D + 1], 1.0)
        nc.vector.memset(zero[:], 0.0).then_inc(v, 1)
        dve.wait_ge(w_in, 32)
        with dve.Fori(0, NT) as i:
            at = i * PREP_STEPS + 1
            dve.wait_ge(node_in, 16 * i + 16)
            norm(h_t[:], at, i + 1).then_inc(v, 1)
            dve.wait_ge(v, at + 5)
            nc.vector.tensor_tensor(z[:], z[:], vec[:, 4, :], ALU.mult).then_inc(v, 1)
            dve.wait_ge(v, at + 6)
            nc.vector.tensor_tensor(z[:], z[:], vec[:, 5, :], ALU.add).then_inc(v, 1)
            dve.wait_ge(v, at + 7)
            nc.vector.tensor_scalar_max(y[:], z[:], 0.0).then_inc(v, 1)
        loads, roots = NT, NT
        for layer in range(LAYERS):
            first = ET * layer
            with dve.Fori(0, ET) as t:
                at = t * EDGE_STEPS + v_at_edges(layer)
                dve.wait_ge(idx_in, 16 * (t + first) + 16)
                nc.vector.tensor_copy(dst_f[:], pair[:, 1:2]).then_inc(v, 1)
                dve.wait_ge(v, at + 1)
                nc.vector.tensor_copy(dst_wide[:], dst_f[:].to_broadcast([P, P])).then_inc(v, 1)
                dve.wait_ge(turned_dst, t + first + 1)
                nc.vector.tensor_scalar(same[:], ps_dst[:], dst_f[:], None, ALU.is_equal).then_inc(v, 1)
                dve.wait_ge(v, at + 3)
                nc.vector.tensor_tensor(before[:], same[:], earlier[:], ALU.mult).then_inc(v, 1)
                dve.wait_ge(v, at + 4)
                nc.vector.tensor_reduce(repeats[:], before[:], AX_X, ALU.max).then_inc(v, 1)
                dve.wait_ge(v, at + 5)
                nc.vector.scalar_tensor_tensor(out=put_f[:], in0=repeats[:], scalar=float(DUMP), in1=dst_f[:],
                                               op0=ALU.mult, op1=ALU.add).then_inc(v, 1)
                dve.wait_ge(v, at + 6)
                nc.vector.tensor_copy(put_idx[:], put_f[:]).then_inc(v, 1)
                dve.wait_ge(summed, t + first + 1)
                dve.wait_ge(old_in, 16 * (t + first) + 16)
                nc.vector.tensor_tensor(new[:], ps_sum[:], old[:], ALU.add).then_inc(v, 1)
            n_in = 3 if layer in (0, 3) else 2
            with dve.Fori(0, NT) as i:
                steps = NODE_STEPS[layer]
                at = i * steps + v_at_nodes(layer)
                dve.wait_ge(node_in, 16 * n_in * i + 16 * (loads + n_in))
                nc.vector.tensor_scalar_max(col[:, 3:4], agg_t[:, D:D + 1], 1.0).then_inc(v, 1)
                dve.wait_ge(v, at + 1)
                nc.vector.reciprocal(col[:, 2:3], col[:, 3:4]).then_inc(v, 1)
                dve.wait_ge(v, at + 2)
                nc.vector.tensor_scalar_mul(mean_t[:], agg_t[:, 0:D], col[:, 2:3]).then_inc(v, 1)
                dve.wait_ge(turn_done, i + NT * layer + 1)
                nc.vector.tensor_copy(turned[:], ps_turn[:]).then_inc(ready, 1)
                dve.wait_ge(proj_done, i + NT * layer + 1)
                nc.vector.tensor_tensor(z[:], ps_out[:], vec[:, layer, :], ALU.add).then_inc(ready, 1)
                dve.wait_ge(ready, 1 + i * 2 + 2 * NT * layer + 2)
                if layer in (1, 2):
                    nc.vector.tensor_scalar_max(y[:], z[:], 0.0).then_inc(v, 1)
                else:
                    nc.vector.tensor_tensor(y[:], z[:], res_t[:], ALU.add).then_inc(v, 1)
                    dve.wait_ge(v, at + 4)
                    nc.vector.tensor_copy(z[:], y[:]).then_inc(v, 1)
                    dve.wait_ge(v, at + 5)
                    nc.vector.bn_stats(stats[:], z[:]).then_inc(v, 1)
                    dve.wait_ge(v, at + 6)
                    nc.vector.memset(spare[:], 0.0)
                    nc.vector.bn_aggr(mv[:], stats[:]).then_inc(v, 1)
                    dve.wait_ge(v, at + 7)
                    nc.vector.tensor_scalar_add(col[:, 0:1], mv[:, 1:2], EPS).then_inc(v, 1)
                    dve.wait_ge(root, i + roots + 1)
                    nc.vector.reciprocal(col[:, 2:3], col[:, 1:2]).then_inc(v, 1)
                    dve.wait_ge(v, at + 9)
                    nc.vector.tensor_scalar(y[:], z[:], mv[:, 0:1], col[:, 2:3], ALU.subtract,
                                            ALU.mult).then_inc(v, 1)
                    dve.wait_ge(v, at + 10)
                    nc.vector.tensor_copy(z[:], y[:]).then_inc(v, 1)
            loads += n_in * NT
            if layer == 0:
                roots += NT

    def tensor(pe):
        pe.wait_ge(ready, 1)
        pe.wait_ge(w_in, 32)
        for layer in range(LAYERS):
            first = ET * layer
            with pe.Fori(0, ET) as t:
                at = t * EDGE_STEPS + v_at_edges(layer)
                pe.wait_ge(v, at + 2)
                nc.tensor.transpose(ps_dst[:], dst_wide[:], ident[:]).then_inc(turned_dst, 1)
                pe.wait_ge(v, at + 3)
                pe.wait_ge(msg_in, 16 * (t + first) + 16)
                nc.tensor.matmul(ps_sum[:], same[:], msg[:], start=True, stop=True).then_inc(summed, 1)
            with pe.Fori(0, NT) as i:
                pe.wait_ge(v, i * NODE_STEPS[layer] + v_at_nodes(layer) + 3)
                for k in range(KH):
                    nc.tensor.transpose(ps_turn[:, 0, k, :], mean_t[:, k * P:(k + 1) * P], ident[:])
                    last = nc.tensor.transpose(ps_turn[:, 1, k, :], h_t[:, k * P:(k + 1) * P], ident[:])
                last.then_inc(turn_done, 1)
                pe.wait_ge(ready, 1 + i * 2 + 2 * NT * layer + 1)
                for side in range(2):
                    for k in range(KH):
                        last = nc.tensor.matmul(ps_out[:], turned[:, side, k, :], w[:, layer, side, k, :],
                                                start=(side == 0 and k == 0), stop=(side == 1 and k == KH - 1))
                last.then_inc(proj_done, 1)

    return {"gpsimd": gpsimd, "sync": sync, "scalar": scalar, "vector": vector, "tensor": tensor}


class Strip:

    def __init__(self, layer, half, odd):
        self.layer, self.half, self.odd = layer, half, odd
        self.s = 2 * half + odd
        self.q = layer * NS + self.s
        self.slot = (layer * NS + odd) % 2
        self.index = 0 if self.is_strip(0) else 3 * self.s - 1

    def is_strip(self, s):
        return isinstance(self.s, int) and self.s == s

    @property
    def parts(self):
        return (0, 1) if self.is_strip(0) else (0, 2) if self.is_strip(NS - 1) else (0, 1, 2)

    def order(self, u):
        return self.index + self.parts.index(u)

    def done_before(self, u):
        return self.layer * NT + self.order(u)

    def tile(self, u):
        return self.s + DT - 1 if u == 2 else (SW // P) * self.s + u

    def turn(self, u):
        return self.s - 1 if u == 2 else self.s

    def next(self):
        return Strip(self.layer, self.half + self.odd, 1 - self.odd)

    def before(self):
        if self.is_strip(0):
            return Strip(self.layer - 1, (NS - 1) // 2, 0) if self.layer else None
        return Strip(self.layer, self.half + self.odd - 1, 1 - self.odd)

    def uses(self, offset):
        return self.half + (offset + self.odd) // 2


PER_PART = (NS, NS - 1, NS - 1)


def finished_at(tile):
    strip = Strip(0, (tile - DT + 1) // 2, (tile - DT + 1) % 2) if tile >= DT else Strip(0, tile // 4, tile // 2 % 2)
    return strip.order(2 if tile >= DT else tile % 2) + 1


def at(h, first, strip, u):
    return h == first + APART * strip.parts.index(u)


def for_strips(eng, layer, body):
    body(Strip(layer, 0, 0))
    body(Strip(layer, 0, 1))
    with eng.Fori(0, (NS - 3) // 2) as k:
        body(Strip(layer, k + 1, 0))
        body(Strip(layer, k + 1, 1))
    body(Strip(layer, (NS - 1) // 2, 0))


def chunk_at(h):
    return range(-(-h * CH // CHUNKS_END), min(CH, -(-(h + 1) * CH // CHUNKS_END)))


def groups_at(h):
    return range(min(SG, SG * h // COUNTS_END), min(SG, SG * (h + 1) // COUNTS_END))


TURN_AT, ROOT_AT, PROJECT_AT, Y_AT, SQRT_AT, APART = 0, 4, 7, 11, 17, 12
COUNTS_END = NT - 3
SUMS_LO_AT = 3
CHUNKS_END, GATHER_OUT_AT = NT - 8, NT - 7
HOT_COL = [sum(CHUNK_WIDTH[:j]) for j in range(CH)]
LEAD = 6
SCALE_SUMS = 1.0 / P
PRODUCTS = ((0, 0), (0, 1), (1, 0))
NORM_LAYERS = {0: 0, LAYERS - 1: 1}


class Fast:

    def __init__(self, nc, mem, shared, features, x, out):
        self.nc, self.mem, self.x, self.out = nc, mem, x, out
        self.sh = shared
        self.a_dram = nc.dram_tensor("f_a_dram", (NS, P, NT * SW), F16, kind="Internal").ap()
        self.x1_dram = nc.dram_tensor("f_x1_dram", (NPAD, D), F32, kind="Internal").ap()
        self.h_dram, self.hp, self.scale, self.c_root = features.h_dram, features.hp, features.scale, features.c_root
        self.h_out = features.h_out
        self.deg_dram = nc.dram_tensor("f_deg_dram", (NPAD,), F32, kind="Internal").ap()
        sb, ps, sem = mem.sb, mem.ps, mem.sem
        self.a_sb = sb("f_a", [P, 2, NT, SW], F16)
        self.hot_key = sb("f_hot_key", [P, HOTS, KW], F16)
        self.hot_lo = sb("f_hot_lo", [P, HOTS, P], F16)
        self.w_dram = features.w_dram
        self.w = sb("f_w", [P, 2, 2, 2, KH, D], F16)
        self.sums = sb("f_sums", [P, KH, SW])
        self.sums_t = sb("f_sums_t", [P, 2, KH, SW], F16)
        self.sums_g = sb("f_sums_g", [P, 2, KH, P], F16)
        self.msg = sb("f_msg", [P, CH, 2 * D], F16)
        self.hot_dst = sb("f_hot_dst", [P, sum(CHUNK_WIDTH)], F16)
        self.idx = sb("f_idx", [P, 2, CH], I32)
        self.pace = sb("f_pace", [P, 2])
        self.root_t = sb("f_root_t", [P, 2, KH, P], F16)
        self.y = sb("f_y", [P, D])
        self.res = sb("f_res", [P, 3, D])
        self.stats = sb("f_stats", [P, 6])
        self.mv = sb("f_mv", [P, 2])
        self.dev = sb("f_dev", [P, 1])
        self.rstd = sb("f_rstd", [P, 1])
        self.carry = sb("f_carry", [P, 1])
        self.deg_n = sb("f_deg_n", [P, NT])
        self.rdeg = sb("f_rdeg", [P, NT])
        self.c_sum = sb("f_c_sum", [P, LAYERS, NT])
        self.ps_agg = ps("f_ps_agg", [P, KH, 512])
        self.ps_gather = ps("f_ps_gather", [P, KH, 512])
        self.ps_build = ps("f_ps_build", [P, 2, 512])
        self.ps_root = ps("f_ps_root", [P, 2, KH, P])
        self.ps_proj = ps("f_ps_proj", [P, 2, D])

        self.deg_out = sem("f_deg_out")
        self.deg_in = sem("f_deg_in")
        self.prep = sem("f_prep")
        self.hot_done = sem("f_hot_done")
        self.counted = sem("f_counted")
        self.a_built = sem("f_a_built")
        self.a_out = [sem(f"f_a_out{b}") for b in range(2)]
        self.a_in = [sem(f"f_a_in{b}") for b in range(2)]
        self.agg_done = sem("f_agg_done")
        self.agg_out = sem("f_agg_out")
        self.idx_ready = sem("f_idx_ready")
        self.paced = sem("f_paced")
        self.msg_in = [sem(f"f_msg_in{i}") for i in range(CH)]
        self.dst_hot = sem("f_dst_hot")
        self.chunk_done = sem("f_chunk_done")
        self.sums_hi = sem("f_sums_hi")
        self.sums_lo = sem("f_sums_lo")
        self.gather_hi = sem("f_gather_hi")
        self.gather_out = sem("f_gather_out")
        self.w_in = sem("f_w_in")
        self.turned = sem("f_turned")
        self.root_out = sem("f_root_out")
        self.proj_done = sem("f_proj_done")
        self.y_part = sem("f_y_part")
        self.y_done = sem("f_y_done")
        self.res_in = [sem(f"f_res_in{b}") for b in range(3)]
        self.res_done = sem("f_res_done")
        self.stat_done = sem("f_stat_done")
        self.var_done = sem("f_var_done")
        self.dev_done = sem("f_dev_done")
        self.rstd_done = sem("f_rstd_done")
        self.z_done = sem("f_z_done")
        self.z_out = [sem(f"f_z_out{b}") for b in range(3)]
        self.hi_done = sem("f_hi_done")
        self.piece_done = sem("f_piece_done")

    def ps_sums(self, strip):
        return self.ps_build if strip.layer and strip.slot else self.ps_agg

    def tensor(self, pe):
        nc, sh = self.nc, self.sh

        def count(strip, g):
            n = strip.s * SG + g
            if g % 2 == 0:
                wait(pe, self.a_built, strip.s * (SG // 2) + g // 2 - 1)
            pe.wait_ge(self.hot_done, 2 * n + 2)
            nc.tensor.matmul(self.ps_build[:, g // 2 % 2, (g % 2) * KW:(g % 2 + 1) * KW],
                             self.hot_lo[:, g % HOTS, :], self.hot_key[:, g % HOTS, :],
                             start=True, stop=True).then_inc(self.counted, 1)

        def turn(strip, u):
            i = strip.tile(u)
            for k in range(KH):
                for part in range(2):
                    last = nc.tensor.matmul(self.ps_root[:, part, k, :],
                                            self.hp[:, strip.layer % 2, i, part, k * P:(k + 1) * P],
                                            sh.ident16[:], start=True, stop=True)
            last.then_inc(self.turned, 1)

        def project(strip, u):
            n = strip.done_before(u)
            if strip.is_strip(0) and u == 0:
                pe.wait_ge(self.w_in, 16 * (strip.layer + 1))
            wait(pe, self.y_done, n)
            if u == 2:
                pe.wait_ge(self.gather_out, strip.layer * (NS - 1) + strip.s)
            else:
                pe.wait_ge(self.sums_lo, strip.q + 1)
            sums = self.sums_g if u == 2 else self.sums_t[:, :, :, u * P:(u + 1) * P]
            for side, own in enumerate((sums, self.root_t)):
                if side == 1:
                    pe.wait_ge(self.root_out, n + 1)
                for i, (part, w_part) in enumerate(PRODUCTS):
                    for k in range(KH):
                        last = nc.tensor.matmul(self.ps_proj[:, side, :], own[:, part, k, :],
                                                self.w[:, strip.layer % 2, w_part, side, k, :],
                                                start=(i == 0 and k == 0),
                                                stop=(i == len(PRODUCTS) - 1 and k == KH - 1))
            last.then_inc(self.proj_done, 1)

        def add_chunk(strip, j):
            m = (strip.layer * (NS - 1) + strip.s - 1) * CH + j
            if j == 0:
                wait(pe, self.gather_out, strip.layer * (NS - 1) + strip.s - 1)
            pe.wait_ge(self.dst_hot, m + 1)
            pe.wait_ge(self.msg_in[j], 16 * (strip.layer * (NS - 1) + strip.s))
            lo_col = CHUNK_BASE[j]
            for k in range(KH):
                for part in range(2):
                    last = nc.tensor.matmul(
                        self.ps_gather[:, k, lo_col:lo_col + CHUNK_WIDTH[j]],
                        self.msg[:, j, part * D + k * P:part * D + (k + 1) * P],
                        self.hot_dst[:, HOT_COL[j]:HOT_COL[j] + CHUNK_WIDTH[j]],
                        start=(j == 0 and part == 0), stop=(j == CH - 1 and part == 1))
            last.then_inc(self.chunk_done, 1)

        def body(strip, dense=True):
            done = strip.before()
            layer, b = strip.layer, strip.slot
            width = P if strip.is_strip(NS - 1) else SW
            for h in range(NT):
                for u in done.parts if done else ():
                    if at(h, TURN_AT, done, u):
                        wait(pe, self.root_out, done.done_before(u))
                        if h == 0:
                            nc.tensor.matmul(self.ps_root[:, 0, 0, :], sh.ident16[:], sh.ident16[:],
                                             start=True, stop=True)
                            turn(done, u)
                if dense and not strip.is_strip(0):
                    for j in chunk_at(h):
                        add_chunk(strip, j)
                if dense:
                    if h == 0:
                        wait(pe, self.agg_out, strip.q - (1 if layer else 0))
                        if layer == 0:
                            pe.wait_ge(self.a_built, (SG // 2) * (strip.s + 1))
                        else:
                            pe.wait_ge(self.a_in[b], 16 * (strip.uses((layer - 1) * NS) + 1))
                    if strip.is_strip(0) and layer:
                        pe.wait_ge(self.piece_done, (layer - 1) * NT + finished_at(h))
                    for k in range(KH):
                        for part in range(2):
                            last = nc.tensor.matmul(
                                self.ps_sums(strip)[:, k, 0:width], self.hp[:, layer % 2, h, part, k * P:(k + 1) * P],
                                self.a_sb[:, b, h, 0:width], start=(h == 0 and part == 0),
                                stop=(h == NT - 1 and part == 1))
                    if h == NT - 1:
                        last.then_inc(self.agg_done, 1)
                for u in done.parts if done else ():
                    if at(h, TURN_AT, done, u) and h:
                        turn(done, u)
                    if at(h, PROJECT_AT, done, u):
                        project(done, u)
                if dense and layer == 0 and not strip.is_strip(NS - 1):
                    for g in groups_at(h):
                        count(strip.next(), g)

        for g in range(SG):
            count(Strip(0, 0, 0), g)
        for layer in range(LAYERS):
            for_strips(pe, layer, body)
        body(Strip(LAYERS, 0, 0), dense=False)

    def scalar(self, act):
        nc, sh = self.nc, self.sh

        def keep(strip, j):
            if j == 0:
                wait(act, self.agg_done, strip.s - 1)
                wait(act, self.a_out[strip.slot], 16 * strip.half)
            act.wait_ge(self.counted, strip.s * SG + 2 * j + 2)
            nc.scalar.activation(self.a_sb[:, strip.slot, :, 2 * GD * j:2 * GD * (j + 1)],
                                 self.ps_build[:, j % 2, 0:2 * KW].rearrange("p (d h) -> p h d", h=NT),
                                 ACT.Copy).then_inc(self.a_built, 1)

        def body(strip, dense=True):
            done = strip.before()
            for h in range(NT):
                if done and h == 0:
                    act.wait_ge(self.agg_done, done.q + 1)
                    wait(act, self.proj_done, done.layer * NT + done.index)
                    nc.scalar.activation(self.sums[:], self.ps_sums(done)[:, :, 0:SW],
                                         ACT.Copy).then_inc(self.agg_out, 1)
                    act.wait_ge(self.agg_out, done.q + 1)
                    nc.scalar.activation(self.sums_t[:, 0], self.sums[:], ACT.Copy,
                                         scale=SCALE_SUMS).then_inc(self.sums_hi, 1)
                for u in done.parts if done else ():
                    n = done.done_before(u)
                    if at(h, ROOT_AT, done, u):
                        act.wait_ge(self.turned, n + 1)
                        wait(act, self.proj_done, n)
                        nc.scalar.activation(self.root_t[:], self.ps_root[:], ACT.Copy).then_inc(self.root_out, 1)
                    if at(h, SQRT_AT, done, u) and done.layer in NORM_LAYERS:
                        act.wait_ge(self.var_done, NORM_LAYERS[done.layer] * NT + done.order(u) + 1)
                        nc.scalar.activation(self.dev[:], self.mv[:, 1:2], ACT.Sqrt,
                                             bias=sh.eps[:]).then_inc(self.dev_done, 1)
                if dense and strip.layer == 0 and not strip.is_strip(NS - 1):
                    for g in groups_at(h):
                        if g % 2:
                            keep(strip.next(), g // 2)
                if dense and h == GATHER_OUT_AT and not strip.is_strip(0):
                    tiles = strip.layer * (NS - 1) + strip.s
                    act.wait_ge(self.chunk_done, CH * tiles)
                    if done:
                        act.wait_ge(self.proj_done, done.layer * NT + done.index + len(done.parts))
                    nc.scalar.activation(self.sums_g[:, 0], self.ps_gather[:, :, 0:P], ACT.Copy,
                                         scale=SCALE_SUMS).then_inc(self.gather_hi, 1)

        for j in range(SG // 2):
            keep(Strip(0, 0, 0), j)
        for layer in range(LAYERS):
            for_strips(act, layer, body)
        body(Strip(LAYERS, 0, 0), dense=False)

    def gpsimd(self, pool):
        nc, sh = self.nc, self.sh

        def gather(strip):
            b = (strip.odd + 1) % 2
            tiles = strip.layer * (NS - 1) + strip.s - 1
            nc.gpsimd.tensor_copy(self.idx[:, b, :], sh.chunk_src[:, bass.ds((strip.s - 1) * CH, CH)]
                                  ).then_inc(self.idx_ready, 1)
            for r, (start, end) in enumerate(SETS):
                pool.wait_ge(self.paced, tiles * len(SETS) + r + 1)
                if r == 0:
                    pool.wait_ge(self.idx_ready, tiles + 1)
                wait(pool, self.chunk_done, (tiles - 1) * CH + end)
                nc.gpsimd.tensor_tensor(self.pace[:, 0:1], self.pace[:, 1:2], self.pace[:, 1:2],
                                        ALU.add).then_inc(self.paced, 1)
                for j in range(start, end):
                    pool.indirect_dma_start(
                        out=self.msg[:, j, :], out_offset=None, in_=self.h_dram[strip.layer],
                        in_offset=bass.IndirectOffsetOnAxis(ap=self.idx[:, b, j:j + 1].bitcast(U32), axis=0)
                    ).then_inc(self.msg_in[j], 16)

        def body(strip):
            if not strip.is_strip(0):
                gather(strip)

        nc.gpsimd.memset(self.pace[:], 0.0).then_inc(self.paced, 1)
        for layer in range(LAYERS):
            pool.wait_ge(self.h_out, 16 * (NT // PT + NT * layer))
            for_strips(pool, layer, body)

    def vector(self, dve):
        nc, sh, vec = self.nc, self.sh, self.sh.vec
        steps = [0]

        def link(ins):
            steps[0] += 1
            ins.then_inc(self.prep, 1)
            dve.wait_ge(self.prep, steps[0])

        def hot(strip, g):
            n = strip.s * SG + g
            wait(dve, self.counted, n - HOTS + 1)
            nc.vector.tensor_scalar(self.hot_key[:, g % HOTS, :], sh.iota[:, 0:KW], sh.key_t[:, bass.ds(n, 1)], None,
                                    ALU.is_equal).then_inc(self.hot_done, 1)
            nc.vector.tensor_scalar(self.hot_lo[:, g % HOTS, :], sh.iota[:, 0:P], sh.lo_t[:, bass.ds(n, 1)], None,
                                    ALU.is_equal).then_inc(self.hot_done, 1)

        def hot_chunk(strip, j):
            m = (strip.layer * (NS - 1) + strip.s - 1) * CH + j
            wait(dve, self.chunk_done, m - CH + 1)
            nc.vector.tensor_scalar(self.hot_dst[:, HOT_COL[j]:HOT_COL[j] + CHUNK_WIDTH[j]], sh.iota[:, 0:CHUNK_WIDTH[j]],
                                    sh.chunk_dst[:, bass.ds((strip.s - 1) * CH + j, 1)], None,
                                    ALU.is_equal).then_inc(self.dst_hot, 1)

        def finish(done, u):
            layer, n, i = done.layer, done.done_before(u), done.tile(u)
            norm = layer in NORM_LAYERS
            m = NORM_LAYERS[layer] * NT + done.order(u) if norm else None
            y, z = self.y[:], self.res[:, u, :]
            if layer < LAYERS - 1:
                hi, lo = (self.hp[:, (layer + 1) % 2, bass.ds(i, 1), part, :].rearrange("p a d -> p (a d)")
                          for part in range(2))

            def neighbours():
                wait(dve, self.piece_done, n if layer < LAYERS - 1 else layer * NT)
                if layer == LAYERS - 1:
                    wait(dve, self.z_done, NT + done.order(u))
                dve.wait_ge(self.proj_done, n + 1)
                nc.vector.scalar_tensor_tensor(out=y, in0=self.ps_proj[:, 0, :],
                                               scalar=self.c_sum[:, layer, bass.ds(i, 1)], in1=vec[:, layer, :],
                                               op0=ALU.mult, op1=ALU.add).then_inc(self.y_part, 1)

            def own():
                dve.wait_ge(self.y_part, n + 1)
                nc.vector.scalar_tensor_tensor(out=y, in0=self.ps_proj[:, 1, :],
                                               scalar=self.c_root[:, layer:layer + 1], in1=y, op0=ALU.mult,
                                               op1=ALU.add).then_inc(self.y_done, 1)

            def residual():
                dve.wait_ge(self.res_in[u], 16 * (NORM_LAYERS[layer] * PER_PART[u] + done.turn(u) + 1))
                dve.wait_ge(self.y_done, n + 1)
                nc.vector.tensor_tensor(y, y, z, ALU.add).then_inc(self.res_done, 1)

            def statistics():
                dve.wait_ge(self.res_done, m + 1)
                nc.vector.bn_stats(self.stats[:], y).then_inc(self.stat_done, 1)

            def variance():
                dve.wait_ge(self.stat_done, m + 1)
                nc.vector.memset(self.carry[:], 0.0)
                nc.vector.bn_aggr(self.mv[:], self.stats[:]).then_inc(self.var_done, 1)

            def deviation():
                dve.wait_ge(self.dev_done, m + 1)
                nc.vector.reciprocal(self.rstd[:], self.dev[:]).then_inc(self.rstd_done, 1)

            def normed():
                dve.wait_ge(self.rstd_done, m + 1)
                nc.vector.tensor_scalar(z, y, self.mv[:, 0:1], self.rstd[:], ALU.subtract,
                                        ALU.mult).then_inc(self.z_done, 1)

            def first_part():
                if norm:
                    dve.wait_ge(self.z_done, m + 1)
                    nc.vector.tensor_scalar(hi, z, self.scale[:, 1:2], None, ALU.mult).then_inc(self.hi_done, 1)
                else:
                    dve.wait_ge(self.y_done, n + 1)
                    nc.vector.tensor_scalar_max(hi, y, 0.0).then_inc(self.hi_done, 1)

            def second_part():
                dve.wait_ge(self.hi_done, n + 1)
                source, factor, op = (z, self.scale[:, 1:2], ALU.mult) if norm else (y, 0.0, ALU.max)
                nc.vector.scalar_tensor_tensor(out=lo, in0=source, scalar=factor, in1=hi, op0=op,
                                               op1=ALU.subtract).then_inc(self.piece_done, 1)

            steps = [neighbours, own]
            if norm:
                steps += [residual, statistics, variance, None, None, deviation, normed]
            if layer < LAYERS - 1:
                steps += [first_part, second_part]
            return steps

        def body(strip, dense=True):
            done = strip.before()
            steps = {u: finish(done, u) for u in done.parts} if done else {}
            for h in range(NT):
                if dense and strip.layer == 0 and not strip.is_strip(NS - 1):
                    for g in groups_at(h):
                        hot(strip.next(), g)
                if dense and not strip.is_strip(0):
                    ahead = list(range(LEAD)) if h == 0 else []
                    for j in ahead + [j + LEAD for j in chunk_at(h) if j + LEAD < CH]:
                        hot_chunk(strip, j)
                if done and h == SUMS_LO_AT:
                    dve.wait_ge(self.sums_hi, done.q + 1)
                    nc.vector.scalar_tensor_tensor(out=self.sums_t[:, 1], in0=self.sums[:], scalar=SCALE_SUMS,
                                                   in1=self.sums_t[:, 0], op0=ALU.mult,
                                                   op1=ALU.subtract).then_inc(self.sums_lo, 1)
                if dense and h == GATHER_OUT_AT + 2 and not strip.is_strip(0):
                    dve.wait_ge(self.gather_hi, strip.layer * (NS - 1) + strip.s)
                    nc.vector.scalar_tensor_tensor(out=self.sums_g[:, 1], in0=self.ps_gather[:, :, 0:P],
                                                   scalar=SCALE_SUMS, in1=self.sums_g[:, 0], op0=ALU.mult,
                                                   op1=ALU.subtract).then_inc(self.gather_out, 1)
                for u in done.parts if done else ():
                    step = h - Y_AT - APART * done.parts.index(u)
                    if 0 <= step < len(steps[u]) and steps[u][step]:
                        steps[u][step]()

        dve.wait_ge(self.deg_in, 16)
        link(nc.vector.tensor_scalar_max(self.rdeg[:], self.deg_n[:], 1.0))
        link(nc.vector.reciprocal(self.deg_n[:], self.rdeg[:]))
        link(nc.vector.tensor_scalar_mul(self.deg_n[:], self.deg_n[:], 1.0 / SCALE_SUMS))
        for layer in range(LAYERS):
            link(nc.vector.tensor_scalar(self.c_sum[:, layer, :], self.deg_n[:], self.c_root[:, layer:layer + 1], None,
                                         ALU.mult))
        for g in range(SG):
            hot(Strip(0, 0, 0), g)
        for layer in range(LAYERS):
            for_strips(dve, layer, body)
        body(Strip(LAYERS, 0, 0), dense=False)

    def sync(self, sp):
        nc = self.nc
        strip_bytes = "p h d -> p (h d)"

        def store_a(strip):
            sp.wait_ge(self.a_built, (SG // 2) * (strip.s + 1))
            sp.dma_start(self.a_dram[bass.ds(strip.s, 1)].rearrange("a p n -> p (a n)"),
                         self.a_sb[:, strip.slot].rearrange(strip_bytes)).then_inc(self.a_out[strip.slot], 16)

        def load_w(layer):
            sp.dma_start(self.w[:, layer % 2].rearrange("p c s k d -> p (c s k d)"),
                         self.w_dram[:, layer]).then_inc(self.w_in, 16)

        def load_a(strip):
            wait(sp, self.agg_done, strip.q - 1)
            sp.dma_start(self.a_sb[:, strip.slot].rearrange(strip_bytes),
                         self.a_dram[bass.ds(strip.s, 1)].rearrange("a p n -> p (a n)")
                         ).then_inc(self.a_in[strip.slot], 16)

        def rows(dram, i):
            return dram[bass.ds(i * P, P), :]

        def body(strip, dense=True):
            done = strip.before()
            layer = strip.layer
            if layer == 1 and strip.is_strip(0):
                sp.wait_ge(self.a_out[0], 16 * ((NS + 1) // 2))
            if dense and layer and not strip.is_strip(NS - 1):
                load_a(strip.next())
            if dense and strip.is_strip(NS - 1) and layer < LAYERS - 1:
                if layer == 0:
                    sp.wait_ge(self.a_out[1], 16 * (NS // 2))
                load_a(Strip(layer + 1, 0, 0))
            if done and done.layer in NORM_LAYERS:
                norm = NORM_LAYERS[done.layer]
                source, target = ((self.x, self.x1_dram), (self.x1_dram, self.out))[norm]
                for u in done.parts:
                    wait(sp, self.z_out[u], 16 * (norm * PER_PART[u] + done.turn(u)))
                    sp.dma_start(self.res[:, u, :], rows(source, done.tile(u))).then_inc(self.res_in[u], 16)
            if strip.is_strip(1) and layer < LAYERS - 1:
                wait(sp, self.proj_done, layer * NT)
                load_w(layer + 1)
            for u in done.parts if done else ():
                if done.layer in NORM_LAYERS:
                    sp.wait_ge(self.z_done, norm * NT + done.order(u) + 1)
                    sp.dma_start(rows(target, done.tile(u)), self.res[:, u, :]).then_inc(self.z_out[u], 16)
                if done.layer < LAYERS - 1:
                    sp.wait_ge(self.piece_done, done.done_before(u) + 1)
                    sp.dma_start(rows(self.h_dram[done.layer + 1], done.tile(u)),
                                 self.hp[:, (done.layer + 1) % 2, bass.ds(done.tile(u), 1)].rearrange(
                                     "p a c d -> p (a c d)")).then_inc(self.h_out, 16)
            if dense and layer == 0 and not strip.is_strip(NS - 1):
                store_a(strip.next())

        load_w(0)
        sp.dma_start(self.deg_dram.rearrange("(c p j) -> p c j", c=GC, p=GP),
                     self.sh.deg[:]).then_inc(self.deg_out, 16)
        sp.wait_ge(self.deg_out, 16)
        with nc.allow_non_contiguous_dma(reason="one degree per partition and node tile"):
            sp.dma_start(self.deg_n[:], self.deg_dram.rearrange("(t p) -> p t", p=P)).then_inc(self.deg_in, 16)
        store_a(Strip(0, 0, 0))
        for layer in range(LAYERS):
            if layer == LAYERS - 1:
                for u in range(3):
                    sp.wait_ge(self.z_out[u], 16 * PER_PART[u])
            for_strips(sp, layer, body)
        body(Strip(LAYERS, 0, 0), dense=False)
        for u in range(3):
            sp.wait_ge(self.z_out[u], 2 * 16 * PER_PART[u])


def build(nc, x, heads, edges, dst_rows, plan, weights, vectors, out):
    with ExitStack() as ctx:
        mem = Mem(nc, ctx)
        sh = Shared(mem)
        with ExitStack() as part:
            features = Features(nc, mem, Mem(nc, part), sh, x, weights)
            find_windows(nc, Mem(nc, part), sh, features, heads, edges, dst_rows, plan, vectors)
        with ExitStack() as part:
            other = general(nc, Mem(nc, part), sh, x, edges, weights, vectors, out)
        fast = Fast(nc, mem, sh, features, x, out)

        block = ctx.enter_context(nc.Block())

        @block.tensor
        def _(pe):
            dense = pe.value_load(sh.dense[:], min_val=0, max_val=1)
            with pe.If(dense):
                fast.tensor(pe)
            with pe.Else():
                other["tensor"](pe)

        @block.scalar
        def _(act):
            dense = act.value_load(sh.dense[:], min_val=0, max_val=1)
            with act.If(dense):
                fast.scalar(act)
            with act.Else():
                other["scalar"](act)

        @block.vector
        def _(dve):
            dense = dve.value_load(sh.dense[:], min_val=0, max_val=1)
            with dve.If(dense):
                fast.vector(dve)
            with dve.Else():
                other["vector"](dve)

        @block.gpsimd
        def _(pool):
            dense = pool.value_load(sh.dense[:], min_val=0, max_val=1)
            with pool.If(dense):
                fast.gpsimd(pool)
            with pool.Else():
                other["gpsimd"](pool)

        @block.sync
        def _(sp):
            dense = sp.value_load(sh.dense[:], min_val=0, max_val=1)
            with sp.If(dense):
                fast.sync(sp)
            with sp.Else():
                other["sync"](sp)


def kernel(**inputs):
    import numpy as np
    import concourse.bacc as bacc
    from concourse import mybir as mb
    from concourse.bass_utils import run_bass_kernel_spmd as run

    def pad_rows(a, rows, fill):
        a = np.asarray(a)
        return np.concatenate([a, np.full((rows - a.shape[0],) + a.shape[1:], fill, a.dtype)])

    sides = [("L0_gnn_W_l", "L0_gnn_W_r")] + [(f"L1_gnn_W{i}l", f"L1_gnn_W{i}r") for i in (1, 2, 3)]
    w = np.stack([np.stack([np.asarray(inputs[n]).T.reshape(KH, P, D) for n in s]) for s in sides])
    w = np.ascontiguousarray(w.transpose(3, 0, 1, 2, 4))
    vec = np.stack([np.asarray(inputs[n]) for n in
                    ("L0_gnn_b_l", "L1_gnn_b1l", "L1_gnn_b2l", "L1_gnn_b3l", "L0_gnn_gamma", "L0_gnn_beta")])
    src, dst = pad_rows(inputs["src"], EPAD, 0), pad_rows(inputs["dst"], EPAD, NPAD - 1)
    past = np.broadcast_to(np.array([0, 1 << 20], src.dtype), (CH * P, 2))
    number = np.arange(CC * GP).reshape(CC, GP).T
    tile_dst, j = (DT + number // CH) * P, number % CH
    plan = np.stack([tile_dst, j, tile_dst + np.array(CHUNK_BASE)[j], np.array(CHUNK_WIDTH)[j]], axis=1)
    arrays = {
        "x": pad_rows(inputs["x"], NPAD, 0),
        "heads": np.ascontiguousarray(np.broadcast_to(dst[::P], (GP, ET))),
        "edges": np.concatenate([np.stack([src, dst], axis=1), past]),
        "dst_rows": dst.reshape(ET, P),
        "plan": np.ascontiguousarray(plan, dtype=np.float32),
        "weights": w,
        "vectors": np.ascontiguousarray(np.broadcast_to(vec, (P,) + vec.shape)),
    }
    nc = bacc.Bacc("TRN2", target_bir_lowering=False, num_devices=1)
    args = [nc.dram_tensor(f"in_{n}_dram", a.shape, mb.dt.from_np(a.dtype), kind="ExternalInput").ap()
            for n, a in arrays.items()]
    out = nc.dram_tensor("out_0_dram", (NPAD, D), F32, kind="ExternalOutput").ap()
    build(nc, *args, out)
    r = run(nc, [{f"in_{n}_dram": a for n, a in arrays.items()}], core_ids=[0])
    return r.results[0]["out_0_dram"][:NODES]
```
